# Optimizing a Trainium2 kernel written in Bass

```python
import numpy as np
import jax
import jax.numpy as jnp

def _softmax(x, axis=-1):
    return jax.nn.softmax(x, axis=axis)
def _gelu(x):
    return jax.nn.gelu(x, approximate=True)
def _silu(x):
    return jax.nn.silu(x)
def _sigmoid(x):
    return jax.nn.sigmoid(x)
def _layernorm(x, axis=-1, eps=1e-5):
    m = jnp.mean(x, axis=axis, keepdims=True)
    v = jnp.var(x, axis=axis, keepdims=True)
    return (x - m) / jnp.sqrt(v + eps)
def _scatter_add(tgt, idx, src, axis=0):
    return tgt.at[idx].add(src)
def _segment_sum(src, seg, n):
    return jax.ops.segment_sum(src, seg, n)

kernel_name = 'mk_conv_seq_d2_conv_nchw512_ab2378'

def setup_inputs(seed: int = 0):
    np.random.seed(seed)
    _w = jnp.asarray
    def _rec_inputs():
        import jax
        import jax.numpy as jnp
        _gk = jax.random.key(seed)
        x = -0.0002928 + 1 * jax.random.normal(jax.random.fold_in(_gk, 1), (8, 512, 32, 32), jnp.float32)
        return x
    x = _rec_inputs()
    def _L0_conv_setup():
        import jax, jax.numpy as jnp
        import numpy as np
        B, C, H, W = (8, 512, 32, 32)
        NUM_HEADS = 8
        GROUPS = min(32, C)
        EPS = 1e-05

        def _group_norm(x, gamma, beta):
            b, c, h, w = x.shape
            xr = x.reshape(b, GROUPS, c // GROUPS, h, w)
            mean = xr.mean(axis=(2, 3, 4), keepdims=True)
            var = xr.var(axis=(2, 3, 4), keepdims=True)
            xr = (xr - mean) * jax.lax.rsqrt(var + EPS)
            x = xr.reshape(b, c, h, w)
            return x * gamma[None, :, None, None] + beta[None, :, None, None]
        key = jax.random.key(seed)
        ks = jax.random.split(key, 7)
        s_qkv = 1.0 / np.sqrt(C)
        s_proj = 1.0 / np.sqrt(C)
        return {'x': jax.random.normal(ks[0], (B, C, H, W), dtype=jnp.float32), 'norm_w': jnp.ones((C,), dtype=jnp.float32), 'norm_b': jnp.zeros((C,), dtype=jnp.float32), 'qkv_w': jax.random.normal(ks[1], (3 * C, C), dtype=jnp.float32) * s_qkv, 'qkv_b': jax.random.normal(ks[2], (3 * C,), dtype=jnp.float32) * 0.01, 'proj_w': jax.random.normal(ks[3], (C, C), dtype=jnp.float32) * s_proj, 'proj_b': jax.random.normal(ks[4], (C,), dtype=jnp.float32) * 0.01}
    _L0_conv_all = _L0_conv_setup()
    _L0_conv_in = {k: v for k, v in _L0_conv_all.items() if k in ('norm_w', 'norm_b', 'qkv_w', 'qkv_b', 'proj_w', 'proj_b', )}
    del _L0_conv_all

    def _L1_conv_setup():
        import jax, jax.numpy as jnp
        import numpy as np
        N_GROUPS = 32
        EPS = 1e-05
        N_HEADS = 8
        D_K = 64

        def _group_norm(x, w, b):
            B, C, H, W = x.shape
            xg = x.reshape(B, N_GROUPS, C // N_GROUPS, H, W)
            mean = xg.mean(axis=(2, 3, 4), keepdims=True)
            var = xg.var(axis=(2, 3, 4), keepdims=True)
            xn = (xg - mean) * jax.lax.rsqrt(var + EPS)
            xn = xn.reshape(B, C, H, W)
            return xn * w[None, :, None, None] + b[None, :, None, None]
        key = jax.random.key(seed)
        ks = jax.random.split(key, 4)
        B, C, H, W = (16, 512, 32, 32)
        x = jax.random.normal(ks[0], (B, C, H, W), dtype=jnp.float32)
        gn_w = jnp.ones((C,), dtype=jnp.float32)
        gn_b = jnp.zeros((C,), dtype=jnp.float32)
        proj_w = jax.random.normal(ks[1], (3 * C, C), dtype=jnp.float32) * C ** (-0.5)
        proj_b = jnp.zeros((3 * C,), dtype=jnp.float32)
        out_w = jax.random.normal(ks[2], (C, C), dtype=jnp.float32) * C ** (-0.5)
        out_b = jnp.zeros((C,), dtype=jnp.float32)
        return {'x': x, 'gn_w': gn_w, 'gn_b': gn_b, 'proj_w': proj_w, 'proj_b': proj_b, 'out_w': out_w, 'out_b': out_b}
    _L1_conv_all = _L1_conv_setup()
    _L1_conv_in = {k: v for k, v in _L1_conv_all.items() if k in ('gn_w', 'gn_b', 'proj_w', 'proj_b', 'out_w', 'out_b', )}
    del _L1_conv_all

    return {
        "x": x,
        "L0_conv_norm_w": _L0_conv_in["norm_w"],
        "L0_conv_norm_b": _L0_conv_in["norm_b"],
        "L0_conv_qkv_w": _L0_conv_in["qkv_w"],
        "L0_conv_qkv_b": _L0_conv_in["qkv_b"],
        "L0_conv_proj_w": _L0_conv_in["proj_w"],
        "L0_conv_proj_b": _L0_conv_in["proj_b"],
        "L1_conv_gn_w": _L1_conv_in["gn_w"],
        "L1_conv_gn_b": _L1_conv_in["gn_b"],
        "L1_conv_proj_w": _L1_conv_in["proj_w"],
        "L1_conv_proj_b": _L1_conv_in["proj_b"],
        "L1_conv_out_w": _L1_conv_in["out_w"],
        "L1_conv_out_b": _L1_conv_in["out_b"],
    }

def reference(x, L0_conv_norm_w, L0_conv_norm_b, L0_conv_qkv_w, L0_conv_qkv_b, L0_conv_proj_w, L0_conv_proj_b, L1_conv_gn_w, L1_conv_gn_b, L1_conv_proj_w, L1_conv_proj_b, L1_conv_out_w, L1_conv_out_b):
    import jax
    import jax.numpy as jnp
    def _L0_conv_ref(x, norm_w, norm_b, qkv_w, qkv_b, proj_w, proj_b):
        import jax, jax.numpy as jnp
        import numpy as np
        B, C, H, W = (8, 512, 32, 32)
        NUM_HEADS = 8
        GROUPS = min(32, C)
        EPS = 1e-05

        def _group_norm(x, gamma, beta):
            b, c, h, w = x.shape
            xr = x.reshape(b, GROUPS, c // GROUPS, h, w)
            mean = xr.mean(axis=(2, 3, 4), keepdims=True)
            var = xr.var(axis=(2, 3, 4), keepdims=True)
            xr = (xr - mean) * jax.lax.rsqrt(var + EPS)
            x = xr.reshape(b, c, h, w)
            return x * gamma[None, :, None, None] + beta[None, :, None, None]
        b, c, h, w = x.shape
        heads = NUM_HEADS
        hd = c // heads
        x_norm = _group_norm(x, norm_w, norm_b)
        qkv = jnp.einsum('bchw,oc->bohw', x_norm, qkv_w) + qkv_b[None, :, None, None]
        qkv = qkv.reshape(b, 3, heads, hd, h * w)
        q, k, v = (qkv[:, 0], qkv[:, 1], qkv[:, 2])
        scale = hd ** (-0.5)
        attn = jnp.einsum('bhdi,bhdj->bhij', q * scale, k)
        attn = jax.nn.softmax(attn, axis=-1)
        out = jnp.einsum('bhij,bhdj->bhdi', attn, v)
        out = out.reshape(b, c, h, w)
        out = jnp.einsum('bchw,oc->bohw', out, proj_w) + proj_b[None, :, None, None]
        return x + out

    def _L1_conv_ref(x, gn_w, gn_b, proj_w, proj_b, out_w, out_b):
        import jax, jax.numpy as jnp
        import numpy as np
        N_GROUPS = 32
        EPS = 1e-05
        N_HEADS = 8
        D_K = 64

        def _group_norm(x, w, b):
            B, C, H, W = x.shape
            xg = x.reshape(B, N_GROUPS, C // N_GROUPS, H, W)
            mean = xg.mean(axis=(2, 3, 4), keepdims=True)
            var = xg.var(axis=(2, 3, 4), keepdims=True)
            xn = (xg - mean) * jax.lax.rsqrt(var + EPS)
            xn = xn.reshape(B, C, H, W)
            return xn * w[None, :, None, None] + b[None, :, None, None]
        B, C, H, W = x.shape
        S = H * W
        scale = D_K ** (-0.25)
        h = _group_norm(x, gn_w, gn_b).reshape(B, C, S).transpose(0, 2, 1)
        qkv = h @ proj_w.T + proj_b
        qkv = qkv.reshape(B, S, N_HEADS, 3 * D_K)
        q, k, v = jnp.split(qkv, 3, axis=-1)
        attn = jnp.einsum('bihd,bjhd->bijh', q * scale, k * scale)
        attn = jax.nn.softmax(attn, axis=2)
        res = jnp.einsum('bijh,bjhd->bihd', attn, v).reshape(B, S, N_HEADS * D_K)
        res = res @ out_w.T + out_b
        res = res.transpose(0, 2, 1).reshape(B, C, H, W)
        return res + x

    def _gn(v, G=32, eps=1e-5):
        B_, C_, H_, W_ = v.shape
        g = v.reshape(B_, G, C_ // G, H_, W_)
        m = jnp.mean(g, axis=(2, 3, 4), keepdims=True)
        s = jnp.var(g, axis=(2, 3, 4), keepdims=True)
        return ((g - m) / jnp.sqrt(s + eps)).reshape(v.shape)

    def _ln_c(v, eps=1e-6):
        m = jnp.mean(v, axis=1, keepdims=True)
        s = jnp.var(v, axis=1, keepdims=True)
        return (v - m) / jnp.sqrt(s + eps)

    def _ln_t(v, eps=1e-5):
        m = jnp.mean(v, axis=-1, keepdims=True)
        s = jnp.var(v, axis=-1, keepdims=True)
        return (v - m) / jnp.sqrt(s + eps)

    def _to_tokens(v):
        B_, C_, H_, W_ = v.shape
        return v.reshape(B_, C_, H_ * W_).transpose(0, 2, 1)
    def _from_tokens(t, like):
        B_, C_, H_, W_ = like.shape
        return t.transpose(0, 2, 1).reshape(B_, C_, H_, W_)

    x = _L0_conv_ref(x, L0_conv_norm_w, L0_conv_norm_b, L0_conv_qkv_w, L0_conv_qkv_b, L0_conv_proj_w, L0_conv_proj_b)
    x = _L1_conv_ref(x, L1_conv_gn_w, L1_conv_gn_b, L1_conv_proj_w, L1_conv_proj_b, L1_conv_out_w, L1_conv_out_b)
    return x


_drawn_inputs = setup_inputs


def setup_inputs(seed=0):
    import zlib

    import numpy as np

    out = dict(_drawn_inputs(seed))
    spreads = {'L0_conv_norm_w': (1.0, 0.2),
     'L0_conv_norm_b': (0.0, 0.1),
     'L1_conv_gn_w': (1.0, 0.2),
     'L1_conv_gn_b': (0.0, 0.1),
     'L1_conv_proj_b': (0.0, 0.1),
     'L1_conv_out_b': (0.0, 0.1)}
    factors = {'L0_conv_qkv_b': 4.014, 'L0_conv_proj_b': 3.96}
    for name, (base, spread) in spreads.items():
        noise = np.random.default_rng([zlib.crc32(name.encode()), seed]).standard_normal(out[name].shape)
        drawn = base * np.exp(spread * noise) if base else spread * noise
        out[name] = jnp.asarray(drawn.astype(out[name].dtype))
    for name, factor in factors.items():
        out[name] = (out[name] * factor).astype(out[name].dtype)
    return out
```

```python
from contextlib import ExitStack

import concourse.bass as bass
import concourse.mybir as mybir

F32 = mybir.dt.float32
F32R = mybir.dt.float32r
ALU = mybir.AluOpType
ACT = mybir.ActivationFunctionType
AX = mybir.AxisListType

C, T = 512, 1024
HEADS, D = 8, 64
P = 128
KT = C // P
JT = T // P
NH = 512
HALVES = T // NH
PAIRS = HEADS // 2
GROUP = C // 32
EPS = 1e-5
SCALE = 1.0 / 8.0

GAMMA, BETA = 0, 4
AHEAD = 11
OWN = 17
BV, BO = 9, 13

STACK = [0, 2, 0, 1, 0, 2, 0, 1]

QK1, QK2, QK3, QK0, WV0, WV1, WO0, WO1 = range(8)
CHUNKS = 8
SLOT = [0, 1, 2, 0, 1, 2, 0, 1]
CHUNK_ROW = {QK0: 0, QK1: 1, QK2: 2, QK3: 3, WV0: 4, WV1: 5, WO0: 6, WO1: 7}
QK_CHUNK = [QK0, QK1, QK2, QK3]
PRO_CHUNKS = [QK0, WV0, WV1]
PRO = len(PRO_CHUNKS)

DRAINED_BY = {"q": "dve", "k": "dve", "max": "dve", "mrow": "act", "den": "act",
              "gm": "dve", "gv": "dve", "v": "act", "out": "dve"}


FOR_ACT, FOR_DVE = ("q", "k", "mrow", "den", "v"), ("max", "gm", "gv", "out")


def qk_items(pair):
    return [(kind, pair, n) for kind in "qk" for n in range(HALVES)]


def max_items(head):
    return [("max", head, i) for i in range(JT * HALVES)]


def spread(items, counts):
    out, at = [], 0
    for c in counts:
        out.append(items[at:at + c])
        at += c
    assert at == len(items)
    return out


STATS_AT = {(4, 4): 0, (4, 6): 1, (5, 6): 2, (6, 0): 3}
GROUP_AT = {(4, 5): [("gm", 0)], (4, 7): [("gv", 0), ("gm", 1)], (5, 1): [("gv", 1)],
            (5, 7): [("gm", 2)], (6, 1): [("gv", 2), ("gm", 3)], (6, 3): [("gv", 3)]}
APPLY_AT = {(5, 2): 0, (5, 3): 1, (6, 2): 2, (6, 4): 3}
RSTD_AT = {(4, 2): [0], (5, 0): [1], (6, 0): [2, 3]}


def unit_steps(last):
    steps = [[[] for _ in range(JT)] for _ in range(HEADS)]
    for h in range(HEADS):
        if h > 0:
            steps[h][1].append(("den", h - 1, 0))
        if last and h == HEADS - 1:
            continue
        if h % 2:
            qk = qk_items((h + 1) // 2)
            steps[h][0] += qk[:2]
            steps[h][1] += qk[2:]
            mx = spread(max_items(h + 1), [0, 0, 4, 3, 3, 3, 3, 0])
        else:
            mx = spread(max_items(h + 1), [3, 3, 2, 2, 2, 2, 2, 0])
        for j in range(JT):
            steps[h][j] += mx[j]
        steps[h][JT - 1] += [("mrow", h + 1, n) for n in range(HALVES)]
    if not last:
        for (h, j), group in GROUP_AT.items():
            steps[h][j] = [(kind, kt, 0) for kind, kt in group] + steps[h][j]
    return steps




def unit_tail(last):
    tail = [("den", HEADS - 1, 0)]
    if not last:
        tail += [("v", t, 0) for t in range(JT)]
    return tail + [("out", m, n) for m in range(KT) for n in range(HALVES)]


def unit_items(last):
    return [i for row in unit_steps(last) for step in row for i in step] + unit_tail(last)


def prologue_items():
    items = []
    for kt in range(KT):
        items += [("gm", kt, 0), ("gv", kt, 0)]
    items += qk_items(0) + [("v", t, 0) for t in range(JT)] + max_items(0) + [("mrow", 0, n) for n in range(HALVES)]
    return items


def drained(items, who):
    return sum(DRAINED_BY[k] == who for k, _, _ in items)


def per_unit(items, kinds):
    return sum(k in kinds for k, _, _ in items)


class Count:

    def __init__(self, first, each):
        self.first, self.each = first, each

    def after(self, u, n):
        return u * self.each + (self.first + n)


def build(nc, x, weights, params, state, units, images):
    loop_items, pro_items = unit_items(False), prologue_items()
    assert len(loop_items) % 2 == 0 and len(pro_items) % 2 == 0

    DRAINED = {who: Count(drained(pro_items, who), drained(loop_items, who)) for who in ("dve", "act")}
    FILLED = {who: Count(per_unit(pro_items, kinds), per_unit(loop_items, kinds))
              for who, kinds in (("act", FOR_ACT), ("dve", FOR_DVE))}
    QKS = Count(4, 16)
    STEPS = Count(0, HEADS * JT)
    ADDS = Count(0, 3 * HEADS)
    HEADC = Count(0, HEADS)
    MAXC = Count(1, HEADS)
    MROWS = Count(2, 2 * HEADS)
    CHUNKC = Count(PRO, CHUNKS)
    GN = Count(KT, KT)
    RESIDS = [Count(0, 16 * len(range(b, KT * HALVES, 3))) for b in range(3)]
    STORES = [Count(16 * len(range(b, images, 3)), RESIDS[b].each) for b in range(3)]
    assert images >= 3

    ctx = ExitStack()

    def sb(name, shape, dt=F32):
        return ctx.enter_context(nc.sbuf_tensor(name, shape, dt))

    def pb(name, shape):
        return ctx.enter_context(nc.psum_tensor(name, shape, F32))

    def sem(name):
        return ctx.enter_context(nc.semaphore(name))

    with ctx:
        x_tile = [sb(f"x_tile{i}", [P, T]) for i in range(2)]
        h_hi = sb("h_hi", [P, KT, T], F32R)
        h_lo = sb("h_lo", [P, KT, T], F32R)
        v_sb = sb("v_sb", [P, JT, C])
        w_stage = [sb(f"w_stage{i}", [P, 1024]) for i in range(2)]
        w_hi = sb("w_hi", [P, 3, 1024], F32R)
        w_lo = sb("w_lo", [P, 3, 1024], F32R)
        q_hh = [sb(f"q_hh{i}", [P, T], F32R) for i in range(3)]
        q_lm = [sb(f"q_lm{i}", [D + 1, T], F32R) for i in range(3)]
        k_hl = [sb(f"k_hl{i}", [P, T], F32R) for i in range(3)]
        k_h1 = [sb(f"k_h1{i}", [D + 1, T], F32R) for i in range(3)]
        probs = [sb(f"probs{i}", [P, T]) for i in range(4)]
        sum_dve = sb("sum_dve", [P, T])
        sum_pool = sb("sum_pool", [P, T])
        dens = sb("dens", [P, NH])
        o_nat = sb("o_nat", [P, T])
        o_hi = sb("o_hi", [P, PAIRS, T], F32R)
        o_lo = sb("o_lo", [P, PAIRS, T], F32R)
        resid = [sb(f"resid{i}", [P, NH]) for i in range(3)]
        ahead = sb("ahead", [P, AHEAD])
        own = sb("own", [P, OWN])
        ident = sb("ident", [P, P])
        ident_r = sb("ident_r", [P, P], F32R)
        group_avg = sb("group_avg", [P, P])
        ones = sb("ones", [P, D])
        mx = sb("mx", [P, JT, HALVES])
        mcol = sb("mcol", [P, JT], F32R)
        stats = sb("stats", [P, HALVES, 6])
        meanvar = sb("meanvar", [P, 2])
        gmean = [sb(f"gmean{i}", [P, 1]) for i in range(2)]
        spread_sq = sb("spread_sq", [P, 1])
        veps = [sb(f"veps{i}", [P, 1]) for i in range(2)]
        rstd = [sb(f"rstd{i}", [P, 1]) for i in range(2)]
        gain = sb("gain", [P, 1])
        minus_half = sb("minus_half", [P, 1])
        pace = sb("pace", [P, 1])
        pool_pace = sb("pool_pace", [P, 1])

        s_ps = [pb(f"s_ps{i}", [P, T]) for i in range(2)]
        work = [pb(f"work{i}", [P, NH]) for i in range(2)]
        o_ps = [pb(f"o_ps{i}", [P, NH]) for i in range(2)]

        x_loaded = [sem(f"x_loaded{i}") for i in range(2)]
        w_loaded = [sem(f"w_loaded{i}") for i in range(2)]
        resid_loaded = [sem(f"resid_loaded{i}") for i in range(3)]
        ahead_loaded = sem("ahead_loaded")
        own_loaded = sem("own_loaded")
        stored = [sem(f"stored{i}") for i in range(3)]
        filled = {"act": sem("filled_for_act"), "dve": sem("filled_for_dve")}
        scores_made = sem("scores_made")
        values_used = sem("values_used")
        act_drained = sem("act_drained")
        hi_made = sem("hi_made")
        exps_done = sem("exps_done")
        o_hi_made = sem("o_hi_made")
        dve_drained = sem("dve_drained")
        gn_scaled = sem("gn_scaled")
        h_hi_made = sem("h_hi_made")
        consts_dve = sem("consts_dve")
        adds_dve = sem("adds_dve")
        maxima_made = sem("maxima_made")
        recips_made = sem("recips_made")
        o_normed = sem("o_normed")
        o_lo_made = sem("o_lo_made")
        mx_parts = sem("mx_parts")
        stats_parts = sem("stats_parts")
        spread_steps = sem("spread_steps")
        gains_made = sem("gains_made")
        stats_made = sem("stats_made")
        spread_made = sem("spread_made")
        h_made = sem("h_made")
        consts_pool = sem("consts_pool")
        masks = sem("masks")
        adds_pool = sem("adds_pool")
        w_hi_made = sem("w_hi_made")
        w_split = sem("w_split")
        rstd_made = sem("rstd_made")

        block = ctx.enter_context(nc.Block())

        def w_tiles(chunk):
            n = 2 if chunk in (WV0, WV1) else 4
            return (w_hi[:, SLOT[chunk], :].rearrange("p (k c) -> p k c", k=n),
                    w_lo[:, SLOT[chunk], :].rearrange("p (k c) -> p k c", k=n))

        def qk_params(kind, pair):
            if pair == 0:
                return ahead, 8 + (kind == "k")
            return own, 3 * (pair - 1) + (kind == "k")

        def over_units(eng, body):
            if units > 1:
                with eng.Fori(0, units - 1) as u:
                    body(u, False)
            body(units - 1, True)

        @block.sync
        def _(sp):
            def load_chunk(n, nth, row, first):
                if not first:
                    sp.wait_ge(w_split, nth)
                sp.dma_start(w_stage[n][:, :], row).then_inc(w_loaded[n], 16)

            sp.dma_start(ahead[:, :], params[0, :, 0:AHEAD]).then_inc(ahead_loaded, 16)
            for kt in range(2):
                sp.dma_start(x_tile[kt][:, :], x[0, kt * P:(kt + 1) * P, :]).then_inc(x_loaded[kt], 16)
            for n in range(2):
                load_chunk((n + 1) % 2, n, weights[0, CHUNK_ROW[PRO_CHUNKS[n]]], True)
            for kt in range(2, KT):
                sp.wait_ge(h_made, kt - 1)
                sp.dma_start(x_tile[kt % 2][:, :], x[0, kt * P:(kt + 1) * P, :]).then_inc(x_loaded[kt % 2], 16)
            load_chunk(1, 1, weights[0, CHUNK_ROW[PRO_CHUNKS[2]]], False)
            for b in range(images):
                sp.dma_start(state[b], x[b]).then_inc(stored[b % 3], 16)

            def unit(u, last):
                def held(value):
                    return value if isinstance(value, int) else sp.snap(value)

                layer, here, made = held(u // images), held(u + 0), held(u + images)
                if not last:
                    after, nxt = held((u + 1) // images), held(u + 1)
                items = unit_items(last)
                splits = [held(CHUNKC.after(u, i - 1)) for i in range(CHUNKS if not last else QK3 + 3)]
                gn_done = [held(GN.after(u, k)) for k in range(3)] if not last else []
                outs = [held(DRAINED["dve"].after(u, drained(items[:items.index(("out", m, n)) + 1], "dve")))
                        for m in range(KT) for n in range(HALVES)]
                stores = [held(STORES[i % 3].after(u, 16 * (i // 3 + 1))) for i in range(KT * HALVES)]
                earlier = [held(STORES[b].after(u, 0)) for b in range(3)]

                def chunk(i):
                    of = after if i in (QK0, WV0, WV1) else layer
                    load_chunk(i % 2, splits[i], weights[of, CHUNK_ROW[i]], False)

                def x_load(kt):
                    sp.dma_start(x_tile[kt % 2][:, :], state[nxt, kt * P:(kt + 1) * P, :]).then_inc(x_loaded[kt % 2], 16)

                def rows(m, n):
                    return (slice(m * P, (m + 1) * P), slice(n * NH, (n + 1) * NH))

                chunk(QK1)
                sp.dma_start(own[:, :], params[layer, :, AHEAD:]).then_inc(own_loaded, 16)
                chunk(QK2)
                chunk(QK3)
                if not last:
                    chunk(QK0)
                    for b in range(3):
                        sp.wait_ge(stored[b], earlier[b])
                    sp.dma_start(ahead[:, :], params[after, :, 0:AHEAD]).then_inc(ahead_loaded, 16)
                    sp.wait_ge(h_made, gn_done[0])
                    x_load(0)
                    x_load(1)
                    chunk(WV0)
                    chunk(WV1)
                    sp.wait_ge(h_made, gn_done[1])
                    x_load(2)
                    sp.wait_ge(h_made, gn_done[2])
                    x_load(3)
                    chunk(WO0)
                    chunk(WO1)
                else:
                    for n, i in enumerate((WO0, WO1)):
                        sp.wait_ge(w_split, splits[QK3 + 1 + n])
                        sp.dma_start(w_stage[(QK3 + 1 + n) % 2][:, :], weights[layer, CHUNK_ROW[i]]).then_inc(
                            w_loaded[(QK3 + 1 + n) % 2], 16)
                def load(i):
                    if i >= 3:
                        sp.wait_ge(stored[i % 3], stores[i - 3])
                    r, c = rows(*divmod(i, HALVES))
                    sp.dma_start(resid[i % 3][:, :], state[here, r, c]).then_inc(resid_loaded[i % 3], 16)

                if last:
                    for b in range(3):
                        sp.wait_ge(stored[b], earlier[b])
                load(0)
                load(1)
                for i in range(KT * HALVES):
                    if i + 2 < KT * HALVES:
                        load(i + 2)
                    r, c = rows(*divmod(i, HALVES))
                    sp.wait_ge(dve_drained, outs[i])
                    sp.dma_start(state[made, r, c], resid[i % 3][:, :]).then_inc(stored[i % 3], 16)
                if last:
                    for i in range(KT * HALVES - 3, KT * HALVES):
                        sp.wait_ge(stored[i % 3], stores[i])

            over_units(sp, unit)

        @block.gpsimd
        def _(pool):
            nc.gpsimd.memset(ident[:, :], 0.0).then_inc(masks, 1)
            nc.gpsimd.memset(group_avg[:, :], 1.0 / GROUP).then_inc(masks, 1)
            nc.gpsimd.memset(ones[:, :], 1.0).then_inc(consts_pool, 1)
            nc.gpsimd.memset(minus_half[:, :], -0.5).then_inc(consts_pool, 1)
            pool.wait_ge(masks, 2)
            nc.gpsimd.affine_select(out=ident[:, :], in_=ident[:, :], compare_op=ALU.not_equal, fill=1.0,
                                    base=0, pattern=[[-1, P]], channel_multiplier=1).then_inc(consts_pool, 1)
            by_group = group_avg[:, :].rearrange("p (g c) -> p g c", c=GROUP)
            nc.gpsimd.affine_select(out=by_group, in_=by_group, compare_op=ALU.is_ge, fill=0.0, base=0,
                                    pattern=[[-GROUP, P // GROUP], [0, GROUP]], channel_multiplier=1).then_inc(masks, 1)
            pool.wait_ge(masks, 3)
            nc.gpsimd.affine_select(out=by_group, in_=by_group, compare_op=ALU.is_ge, fill=0.0, base=GROUP - 1,
                                    pattern=[[GROUP, P // GROUP], [0, GROUP]], channel_multiplier=-1).then_inc(consts_pool, 1)
            pool.wait_ge(consts_pool, 4)

            def split(chunk, stage, nth, loads):
                pool.wait_ge(w_loaded[stage], loads)
                nc.gpsimd.tensor_tensor(pool_pace[:, :], minus_half[:, :], minus_half[:, :], ALU.add)
                nc.gpsimd.tensor_copy(w_hi[:, SLOT[chunk], :], w_stage[stage][:, :]).then_inc(w_hi_made, 1)
                pool.wait_ge(w_hi_made, nth + 1)
                nc.gpsimd.tensor_tensor(w_lo[:, SLOT[chunk], :], w_stage[stage][:, :],
                                        w_hi[:, SLOT[chunk], :].bitcast(F32), ALU.subtract).then_inc(w_split, 1)

            def rstd_of(kt, drained_to):
                pool.wait_ge(dve_drained, drained_to)
                nc.gpsimd.tensor_tensor(rstd[kt % 2][:, :], veps[kt % 2][:, :], minus_half[:, :], ALU.pow).then_inc(rstd_made, 1)

            split(QK0, 1, 0, 16)
            split(WV0, 0, 1, 16)
            for kt in range(KT):
                rstd_of(kt, drained(pro_items[:pro_items.index(("gv", kt, 0)) + 1], "dve"))
            split(WV1, 1, 2, 32)

            def unit(u, last):
                items = unit_items(last)

                def split_here(i, place=None):
                    place = i if place is None else place
                    stage = place % 2
                    loads = Count(16 * (1 + stage), 64).after(u, 16 * (place // 2 + 1))
                    if i in (QK1, QK2, QK3):
                        pool.wait_ge(filled["act"], FILLED["act"].after(u, 0))
                        pool.wait_ge(filled["dve"], FILLED["dve"].after(u, 0))
                    else:
                        user = {QK0: ("k", 1, 1), WV0: ("k", 2, 1), WV1: ("k", 3, 1),
                                WO0: ("k", 1 if last else 4, 1), WO1: ("k", 2, 1) if last else ("v", JT - 1, 0)}[i]
                        upto = items[:items.index(user) + 1]
                        pool.wait_ge(filled["act"], FILLED["act"].after(u, per_unit(upto, FOR_ACT)))
                    split(i, stage, CHUNKC.after(u, place), loads)

                def add(h, k):
                    j = 2 * k + 3
                    if k == 0 and h > 0:
                        upto = items[:items.index(("den", h - 1, 0)) + 1]
                        pool.wait_ge(filled["act"], FILLED["act"].after(u, per_unit(upto, FOR_ACT)))
                    if k > 0:
                        pool.wait_ge(adds_pool, ADDS.after(u, 3 * h + k))
                    pool.wait_ge(exps_done, STEPS.after(u, h * JT + j + 1))
                    first = probs[1] if k == 0 else sum_pool
                    nc.gpsimd.tensor_tensor(sum_pool[:, :], first[:, :], probs[j % 4][:, :], ALU.add).then_inc(adds_pool, 1)

                before = {0: QK1, 1: QK2, 2: QK3}
                if not last:
                    before.update({3: QK0, 4: WV0, 6: WV1})
                for h in range(HEADS):
                    if h in before:
                        split_here(before[h])
                    for k in range(3):
                        if not last:
                            for kt in RSTD_AT.get((h, k), []):
                                upto = items[:items.index(("gv", kt, 0)) + 1]
                                rstd_of(kt, DRAINED["dve"].after(u, drained(upto, "dve")))
                        add(h, k)
                if not last:
                    split_here(WO0)
                    split_here(WO1)
                else:
                    split_here(WO0, QK3 + 1)
                    split_here(WO1, QK3 + 2)

            over_units(pool, unit)

        @block.scalar
        def _(act):
            def filled_of(kinds_items, item):
                upto = kinds_items[:kinds_items.index(item) + 1]
                return per_unit(upto, FOR_ACT)

            def qk_hi(item, bank, heads, col, par):
                kind, _, n = item
                for half, s in enumerate(heads):
                    rows = slice(half * D, (half + 1) * D)
                    src, bias = work[bank][rows, :], par[rows, col:col + 1]
                    cols = slice(n * NH, (n + 1) * NH)
                    if kind == "q":
                        outs = (q_hh[s][0:D, cols], q_hh[s][D:P, cols])
                    else:
                        outs = (k_hl[s][0:D, cols], k_h1[s][0:D, cols])
                    for k, out in enumerate(outs):
                        done = nc.scalar.activation(out, src, ACT.Identity, bias=bias)
                        if half == 1 and k == 1:
                            done.then_inc(hi_made, 1)

            def mrow(item, bank, s):
                n = item[2]
                nc.scalar.activation(q_lm[s][D:D + 1, n * NH:(n + 1) * NH], work[bank][0:1, :], ACT.Copy,
                                     scale=-1.0).then_inc(act_drained, 1)

            def take(items, item, at):
                kind, a, n = item
                bank = items.index(item) % 2
                act.wait_ge(filled["act"], at(filled_of(items, item)))
                if kind in "qk":
                    pair = a % PAIRS
                    par, col = qk_params(kind, pair)
                    qk_hi(item, bank, (STACK[2 * pair], STACK[2 * pair + 1]), col, par)
                elif kind == "mrow":
                    mrow(item, bank, STACK[a % HEADS])
                elif kind == "den":
                    nc.scalar.copy(dens[:, :], work[bank][:, :]).then_inc(act_drained, 1)
                else:
                    nc.scalar.copy(v_sb[:, a, :], work[bank][:, :]).then_inc(act_drained, 1)

            act.wait_ge(ahead_loaded, 16)
            for item in pro_items:
                if item[0] in FOR_ACT:
                    take(pro_items, item, lambda n: n)

            def unit(u, last):
                items, steps = unit_items(last), unit_steps(last)

                def at(n):
                    return FILLED["act"].after(u, n)

                def o_high(h):
                    rows = slice(h % 2 * D, (h % 2 + 1) * D)
                    act.wait_ge(o_normed, HEADC.after(u, h + 1))
                    nc.scalar.activation(o_hi[rows, h // 2, :], o_nat[rows, :], ACT.Identity,
                                         bias=own[rows, BV + h // 2:BV + h // 2 + 1]).then_inc(o_hi_made, 1)

                def exp(h, j):
                    act.wait_ge(scores_made, STEPS.after(u, h * JT + j + 1))
                    if h > 0 or j >= 4:
                        act.wait_ge(values_used, STEPS.after(u, h * JT + j - 3))
                        mine = adds_pool if j % 2 else adds_dve
                        need = {4: 3 * h + 1, 5: 3 * h + 1, 0: 3 * h - 1, 1: 3 * h - 1, 2: 3 * h, 3: 3 * h}.get(j)
                        if need is not None:
                            act.wait_ge(mine, ADDS.after(u, need))
                    nc.scalar.activation(probs[j % 4][:, :], s_ps[j % 2][:, :], ACT.Exp, scale=SCALE).then_inc(exps_done, 1)

                for h in range(HEADS):
                    if h == 1:
                        act.wait_ge(own_loaded, Count(0, 16).after(u, 16))
                    if h == HEADS - 1 and not last:
                        act.wait_ge(ahead_loaded, Count(16, 16).after(u, 16))
                    for j in range(JT):
                        if j < JT - 1:
                            exp(h, j)
                        for item in steps[h][j]:
                            if item[0] in ("q", "k", "mrow", "den"):
                                take(items, item, at)
                        if j == JT - 1:
                            exp(h, j)
                        if j == 7 and h > 0:
                            o_high(h - 1)
                for item in unit_tail(last):
                    if item[0] in ("den", "v"):
                        take(items, item, at)
                    if item == ("v", 1, 0):
                        o_high(HEADS - 1)
                if last:
                    o_high(HEADS - 1)

            over_units(act, unit)

        @block.vector
        def _(dve):
            v = nc.vector

            def filled_of(items, item):
                upto = items[:items.index(item) + 1]
                return per_unit(upto, FOR_DVE)

            def qks_of(items, item):
                upto = items[:items.index(item) + 1]
                return per_unit(upto, ("q", "k"))

            def qk_lo(item, bank, heads, col, par):
                kind, _, n = item
                cols = slice(n * NH, (n + 1) * NH)
                for half, s in enumerate(heads):
                    rows = slice(half * D, (half + 1) * D)
                    src = work[bank][rows, :]
                    if kind == "q":
                        hi, bias, out = q_hh[s][rows, cols], par[rows, col:col + 1], q_lm[s][0:D, cols]
                    else:
                        hi, bias, out = k_hl[s][0:D, cols], par[0:D, col + half:col + half + 1], k_hl[s][D:P, cols]
                    done = v.scalar_tensor_tensor(out=out, in0=src, scalar=bias, in1=hi.bitcast(F32),
                                                  op0=ALU.add, op1=ALU.subtract)
                done.then_inc(dve_drained, 1)

            def gn_stats(kt, nth_load, nth):
                dve.wait_ge(x_loaded[kt % 2], nth_load)
                for n in range(HALVES):
                    v.bn_stats(stats[:, n, :], x_tile[kt % 2][:, n * NH:(n + 1) * NH]).then_inc(stats_parts, 1)
                dve.wait_ge(stats_parts, 2 * nth + 2)
                v.memset(pace[:, :], 0.0)
                v.bn_aggr(meanvar[:, :], stats[:, :, :]).then_inc(stats_made, 1)

            def gn_mean(kt, bank, nth):
                v.tensor_tensor(spread_sq[:, :], meanvar[:, 0:1], work[bank][:, 0:1], ALU.subtract).then_inc(spread_steps, 1)
                v.tensor_copy(gmean[kt % 2][:, :], work[bank][:, 0:1]).then_inc(dve_drained, 1)
                dve.wait_ge(spread_steps, 2 * nth + 1)
                v.tensor_tensor(spread_sq[:, :], spread_sq[:, :], spread_sq[:, :], ALU.mult).then_inc(spread_steps, 1)
                dve.wait_ge(spread_steps, 2 * nth + 2)
                v.tensor_tensor(spread_sq[:, :], spread_sq[:, :], meanvar[:, 1:2], ALU.add).then_inc(spread_made, 1)

            def gn_var(kt, bank):
                done = v.tensor_scalar(veps[kt % 2][:, :], work[bank][:, 0:1], EPS, None, ALU.add)
                done.then_inc(dve_drained, 1)

            def gn_apply(kt, nth):
                dve.wait_ge(rstd_made, nth + 1)
                v.tensor_tensor(gain[:, :], rstd[kt % 2][:, :], ahead[:, GAMMA + kt:GAMMA + kt + 1], ALU.mult).then_inc(gains_made, 1)
                dve.wait_ge(gains_made, nth + 1)
                v.tensor_scalar(x_tile[kt % 2][:, :], x_tile[kt % 2][:, :], gmean[kt % 2][:, :], gain[:, :],
                                ALU.subtract, ALU.mult).then_inc(gn_scaled, 1)
                beta = ahead[:, BETA + kt:BETA + kt + 1]
                dve.wait_ge(gn_scaled, nth + 1)
                v.tensor_scalar(h_hi[:, kt, :], x_tile[kt % 2][:, :], beta, None, ALU.add).then_inc(h_hi_made, 1)
                dve.wait_ge(h_hi_made, nth + 1)
                v.scalar_tensor_tensor(out=h_lo[:, kt, :], in0=x_tile[kt % 2][:, :], scalar=beta,
                                       in1=h_hi[:, kt, :].bitcast(F32), op0=ALU.add, op1=ALU.subtract).then_inc(h_made, 1)

            def maximum(item, bank, nth_head):
                t, n = divmod(item[2], HALVES)
                ins = v.reduce_max(mx[:, t, n:n + 1], work[bank][:, :], axis=AX.X)
                ins.then_inc(dve_drained, 1)

            def maxima(drained_to, nth):
                dve.wait_ge(dve_drained, drained_to)
                v.tensor_tensor(mcol[:, :], mx[:, :, 0], mx[:, :, 1], ALU.max).then_inc(maxima_made, 1)

            def take(items, item, at, u):
                kind, a, n = item
                bank = items.index(item) % 2
                upto = drained(items[:items.index(item) + 1], "dve")
                if kind in "qk":
                    pair = a % PAIRS
                    par, col = qk_params(kind, pair)
                    dve.wait_ge(hi_made, at("qk", qks_of(items, item)))
                    qk_lo(item, bank, (STACK[2 * pair], STACK[2 * pair + 1]), col, par)
                    return
                dve.wait_ge(filled["dve"], at("filled", filled_of(items, item)))
                if kind == "max":
                    maximum(item, bank, None)
                    if n == JT * HALVES - 1:
                        maxima(at("drained", upto), None)
                elif kind == "gm":
                    gn_mean(a, bank, at("gn", a))
                elif kind == "gv":
                    gn_var(a, bank)
                elif kind == "out":
                    i = a * HALVES + n
                    dve.wait_ge(resid_loaded[i % 3], RESIDS[i % 3].after(u, 16 * (i // 3 + 1)))
                    done = v.scalar_tensor_tensor(out=resid[i % 3][:, :], in0=work[bank][:, :],
                                                  scalar=own[:, BO + a:BO + a + 1], in1=resid[i % 3][:, :],
                                                  op0=ALU.add, op1=ALU.add)
                    done.then_inc(dve_drained, 1)

            def before_loop(what, n):
                return n

            for s in range(3):
                v.memset(k_h1[s][D:D + 1, :].bitcast(F32), 1.0).then_inc(consts_dve, 1)
            dve.wait_ge(consts_pool, 4)
            v.tensor_copy(ident_r[:, :], ident[:, :]).then_inc(consts_dve, 1)
            dve.wait_ge(ahead_loaded, 16)
            for kt in range(KT):
                gn_stats(kt, 16 * (kt // 2 + 1), kt)
                take(pro_items, ("gm", kt, 0), before_loop, 0)
                take(pro_items, ("gv", kt, 0), before_loop, 0)
                gn_apply(kt, kt)
            for item in pro_items:
                if item[0] in ("q", "k", "max"):
                    take(pro_items, item, before_loop, 0)

            def unit(u, last):
                items, steps = unit_items(last), unit_steps(last)

                def at(what, n):
                    return {"qk": QKS, "filled": FILLED["dve"], "drained": DRAINED["dve"], "gn": GN}[what].after(u, n)

                def add(h, k):
                    j = 2 * k + 2
                    if k > 0:
                        dve.wait_ge(adds_dve, ADDS.after(u, 3 * h + k))
                    dve.wait_ge(exps_done, STEPS.after(u, h * JT + j + 1))
                    first = probs[0] if k == 0 else sum_dve
                    v.tensor_tensor(sum_dve[:, :], first[:, :], probs[j % 4][:, :], ALU.add).then_inc(adds_dve, 1)

                def reciprocal(h, piece):
                    if piece == 0:
                        upto = items[:items.index(("den", h, 0)) + 1]
                        dve.wait_ge(act_drained, DRAINED["act"].after(u, drained(upto, "act")))
                    cols = slice(piece * P, (piece + 1) * P)
                    v.reciprocal(dens[:, cols], dens[:, cols]).then_inc(recips_made, 1)

                def normalize(h):
                    dve.wait_ge(recips_made, Count(0, 4 * HEADS).after(u, 4 * h + 4))
                    for half in range(HALVES):
                        rows = slice(half * D, (half + 1) * D)
                        done = v.tensor_tensor(o_nat[h % 2 * D:(h % 2 + 1) * D, half * NH:(half + 1) * NH],
                                               o_ps[h % 2][rows, :], dens[rows, :], ALU.mult)
                    done.then_inc(o_normed, 1)

                def o_low(h):
                    rows = slice(h % 2 * D, (h % 2 + 1) * D)
                    dve.wait_ge(o_hi_made, HEADC.after(u, h + 1))
                    v.scalar_tensor_tensor(out=o_lo[rows, h // 2, :], in0=o_nat[rows, :],
                                           scalar=own[rows, BV + h // 2:BV + h // 2 + 1],
                                           in1=o_hi[rows, h // 2, :].bitcast(F32),
                                           op0=ALU.add, op1=ALU.subtract).then_inc(o_lo_made, 1)

                for h in range(HEADS):
                    if h == 1:
                        dve.wait_ge(own_loaded, Count(0, 16).after(u, 16))
                    if h == 5 and not last:
                        dve.wait_ge(ahead_loaded, Count(16, 16).after(u, 16))
                    for j in range(JT):
                        if not last and (h, j) in STATS_AT:
                            kt = STATS_AT[h, j]
                            gn_stats(kt, Count(32, 32).after(u, 16 * (kt // 2 + 1)), GN.after(u, kt))
                        for item in steps[h][j]:
                            if DRAINED_BY[item[0]] == "dve":
                                take(items, item, at, u)
                        if not last and (h, j) in APPLY_AT:
                            kt = APPLY_AT[h, j]
                            gn_apply(kt, GN.after(u, kt))
                        if j in (3, 5, 7):
                            add(h, (j - 3) // 2)
                        if h > 0 and 2 <= j <= 5:
                            reciprocal(h - 1, j - 2)
                        if h > 0 and j == 6:
                            normalize(h - 1)
                        if h > 1 and j == 0:
                            o_low(h - 2)
                o_low(HEADS - 2)
                for piece in range(4):
                    reciprocal(HEADS - 1, piece)
                normalize(HEADS - 1)
                o_low(HEADS - 1)
                for item in unit_tail(last):
                    if item[0] == "out":
                        take(items, item, at, u)

            over_units(dve, unit)

        @block.tensor
        def _(pe):
            mm = nc.tensor.matmul

            def three(out, w, x, k, n, flip=False):
                (wh, wl), (xh, xl) = w, x
                pairs = [(xh, wh), (xh, wl), (xl, wh)] if flip else [(wh, xh), (wl, xh), (wh, xl)]
                for i, (a, b) in enumerate(pairs):
                    last = mm(out, a, b, start=(k == 0 and i == 0), stop=(k == n - 1 and i == 2))
                return last

            def fill(items, item, prior, u):
                kind, a, n = item
                pos = items.index(item)
                bank = work[pos % 2]
                if pos < 2:
                    if prior is not None:
                        pe.wait_ge(dve_drained, prior("dve", 0))
                        pe.wait_ge(act_drained, prior("act", 0))
                else:
                    who = DRAINED_BY[items[pos - 2][0]]
                    upto = drained(items[:pos - 1], who)
                    pe.wait_ge(dve_drained if who == "dve" else act_drained, upto if prior is None else prior(who, upto))
                if kind in "qk":
                    wh, wl = w_tiles(QK_CHUNK[a % PAIRS])
                    cols = slice(0, P) if kind == "q" else slice(P, 2 * P)
                    for k in range(KT):
                        last = three(bank[:, :], (wh[:, k, cols], wl[:, k, cols]),
                                     (h_hi[:, k, n * NH:(n + 1) * NH], h_lo[:, k, n * NH:(n + 1) * NH]), k, KT)
                    last.then_inc(filled["act"], 1)
                elif kind == "max":
                    s = STACK[a % HEADS]
                    t, half = divmod(n, HALVES)
                    mm(bank[:, :], q_hh[s][0:D, t * P:(t + 1) * P], k_hl[s][0:D, half * NH:(half + 1) * NH],
                       start=True, stop=True).then_inc(filled["dve"], 1)
                elif kind == "mrow":
                    for t in range(JT // HALVES):
                        last = mm(bank[0:1, t * P:(t + 1) * P], mcol[:, n * 4 + t:n * 4 + t + 1], ident_r[:, :],
                                  start=True, stop=True)
                    last.then_inc(filled["act"], 1)
                elif kind == "den":
                    for half in range(HALVES):
                        out, cols = bank[half * D:(half + 1) * D, :], slice(half * NH, (half + 1) * NH)
                        mm(out, ones[:, :], sum_dve[:, cols], start=True, stop=False)
                        last = mm(out, ones[:, :], sum_pool[:, cols], start=False, stop=True)
                    last.then_inc(filled["act"], 1)
                elif kind == "gm":
                    mm(bank[:, 0:1], group_avg[:, :], meanvar[:, 0:1], start=True, stop=True).then_inc(filled["dve"], 1)
                elif kind == "gv":
                    mm(bank[:, 0:1], group_avg[:, :], spread_sq[:, :], start=True, stop=True).then_inc(filled["dve"], 1)
                elif kind == "v":
                    for k in range(KT):
                        wh, wl = w_tiles(WV0 if k < 2 else WV1)
                        tok = slice(a * P, (a + 1) * P)
                        last = three(bank[:, :], (wh[:, k % 2, :], wl[:, k % 2, :]),
                                     (h_hi[:, k, tok], h_lo[:, k, tok]), k, KT, flip=True)
                    last.then_inc(filled["act"], 1)
                elif kind == "out":
                    wh, wl = w_tiles(WO0 if a < 2 else WO1)
                    cols = slice(a % 2 * P, (a % 2 + 1) * P)
                    for k in range(KT):
                        half = slice(n * NH, (n + 1) * NH)
                        last = three(bank[:, :], (wh[:, k, cols], wl[:, k, cols]), (o_hi[:, k, half], o_lo[:, k, half]), k, KT)
                    last.then_inc(filled["dve"], 1)

            pe.wait_ge(consts_pool, 4)
            pe.wait_ge(consts_dve, 4)
            for item in pro_items:
                kind, a, n = item
                if kind == "gm":
                    pe.wait_ge(stats_made, a + 1)
                elif kind == "gv":
                    pe.wait_ge(spread_made, a + 1)
                elif kind == "q" and n == 0:
                    pe.wait_ge(h_made, KT)
                    pe.wait_ge(w_split, PRO)
                elif kind == "max" and n == 0:
                    pe.wait_ge(dve_drained, drained(pro_items[:pro_items.index(item)], "dve"))
                elif kind == "mrow" and n == 0:
                    pe.wait_ge(maxima_made, 1)
                fill(pro_items, item, None, 0)

            def unit(u, last):
                items, steps = unit_items(last), unit_steps(last)

                def prior(who, n):
                    return DRAINED[who].after(u, n)

                def scores(h, j):
                    g, s = h * JT + j, STACK[h]
                    if j >= 2 or h > 0:
                        pe.wait_ge(exps_done, STEPS.after(u, g - 1))
                    if j == 0:
                        at = prologue_or(items, h)
                        pe.wait_ge(act_drained, DRAINED["act"].after(u, at))
                    keys = slice(j * P, (j + 1) * P)
                    for n in range(HALVES):
                        half = slice(n * NH, (n + 1) * NH)
                        mm(s_ps[j % 2][:, half], k_hl[s][:, keys], q_hh[s][:, half], start=True, stop=False)
                    for n in range(HALVES):
                        half = slice(n * NH, (n + 1) * NH)
                        done = mm(s_ps[j % 2][:, half], k_h1[s][:, keys], q_lm[s][:, half], start=False, stop=True)
                    done.then_inc(scores_made, 1)

                def values(h, j):
                    pe.wait_ge(exps_done, STEPS.after(u, h * JT + j + 1))
                    if j == 0 and h >= 2:
                        pe.wait_ge(o_normed, HEADC.after(u, h - 1))
                    for half in range(HALVES):
                        done = mm(o_ps[h % 2][half * D:(half + 1) * D, :], v_sb[:, j, h * D:(h + 1) * D],
                                  probs[j % 4][:, half * NH:(half + 1) * NH], start=(j == 0), stop=(j == JT - 1))
                    done.then_inc(values_used, 1)

                def ready(item):
                    kind, a, n = item
                    if kind == "gm":
                        pe.wait_ge(stats_made, GN.after(u, a + 1))
                    elif kind == "gv":
                        pe.wait_ge(spread_made, GN.after(u, a + 1))
                    elif kind == "q" and n == 0:
                        chunk = QK_CHUNK[a % PAIRS]
                        pe.wait_ge(w_split, CHUNKC.after(u, chunk + 1))
                        if a == PAIRS:
                            pe.wait_ge(h_made, GN.after(u, KT))
                    elif kind == "max" and n == 0 and a % 2 == 0:
                        upto = items[:items.index(("k", a // 2, HALVES - 1)) + 1]
                        pe.wait_ge(dve_drained, DRAINED["dve"].after(u, drained(upto, "dve")))
                    elif kind == "mrow" and n == 0:
                        pe.wait_ge(maxima_made, MAXC.after(u, a))
                    elif kind == "den":
                        pe.wait_ge(adds_dve, ADDS.after(u, 3 * a + 3))
                        pe.wait_ge(adds_pool, ADDS.after(u, 3 * a + 3))
                    elif kind == "v" and a == 0:
                        pe.wait_ge(w_split, CHUNKC.after(u, WV1 + 1))
                    elif kind == "out" and n == 0 and a % 2 == 0:
                        if a == 0:
                            pe.wait_ge(o_lo_made, HEADC.after(u, HEADS))
                        place = (WO0 if a == 0 else WO1) if not last else QK3 + 1 + a // 2
                        pe.wait_ge(w_split, CHUNKC.after(u, place + 1))

                for h in range(HEADS):
                    for j in range(JT):
                        rows = steps[h][j]
                        if j == JT - 1:
                            for item in rows:
                                ready(item)
                                fill(items, item, prior, u)
                        scores(h, j)
                        if j > 0:
                            values(h, j - 1)
                        elif h > 0:
                            values(h - 1, JT - 1)
                        if j < JT - 1:
                            for item in rows:
                                ready(item)
                                fill(items, item, prior, u)
                values(HEADS - 1, JT - 1)
                for item in unit_tail(last):
                    ready(item)
                    fill(items, item, prior, u)

            def prologue_or(items, h):
                if h == 0:
                    return 0
                return drained(items[:items.index(("mrow", h, HALVES - 1)) + 1], "act")

            over_units(pe, unit)


_WEIGHTS = ("L0_conv_qkv_w", "L0_conv_proj_w", "L1_conv_proj_w", "L1_conv_out_w")


def lay_out(inputs):
    import numpy as np

    def f(name):
        return np.asarray(inputs[name])

    w1 = f("L1_conv_proj_w").reshape(HEADS, 3, D, C).transpose(1, 0, 2, 3).reshape(3 * C, C)
    b1 = f("L1_conv_proj_b").reshape(HEADS, 3, D).transpose(1, 0, 2).reshape(3 * C)
    layers = [
        (f("L0_conv_norm_w"), f("L0_conv_norm_b"), f("L0_conv_qkv_w"), f("L0_conv_qkv_b"), f("L0_conv_proj_w"), f("L0_conv_proj_b")),
        (f("L1_conv_gn_w"), f("L1_conv_gn_b"), w1, b1, f("L1_conv_out_w"), f("L1_conv_out_b")),
    ]
    weights = np.zeros((2, 8, P, 1024), np.float32)
    params = np.zeros((2, P, AHEAD + OWN), np.float32)
    for n, (gamma, beta, wqkv, bqkv, wo, bo) in enumerate(layers):
        wt = wqkv.T.reshape(KT, P, 3, C)
        for p in range(PAIRS):
            qk = wt[:, :, 0:2, p * P:(p + 1) * P]
            weights[n, p] = qk.transpose(1, 0, 2, 3).reshape(P, 1024)
        for i in range(2):
            weights[n, 4 + i] = wt[2 * i:2 * i + 2, :, 2, :].transpose(1, 0, 2).reshape(P, 1024)
            weights[n, 6 + i] = wo.T.reshape(KT, P, 2, 256)[:, :, i].transpose(1, 0, 2).reshape(P, 1024)
        bq, bk, bv = bqkv.reshape(3, PAIRS, P)
        params[n, :, GAMMA:GAMMA + KT] = gamma.reshape(KT, P).T
        params[n, :, BETA:BETA + KT] = beta.reshape(KT, P).T
        for p in range(PAIRS):
            at = 8 if p == 0 else AHEAD + 3 * (p - 1)
            params[n, :, at] = bq[p]
            params[n, :, at + 1] = bk[p]
            params[n, :D, at + 2] = bk[p, D:]
            params[n, D:, at + 2] = bk[p, :D]
        params[n, :, AHEAD + BV:AHEAD + BV + PAIRS] = bv.T
        params[n, :, AHEAD + BO:AHEAD + BO + KT] = bo.reshape(KT, P).T
    return weights, params


def kernel(**inputs):
    import numpy as np
    import concourse.bacc as bacc
    from concourse.bass_utils import run_bass_kernel_spmd as run

    x = np.asarray(inputs["x"])
    images = x.shape[0]
    weights, params = lay_out(inputs)
    arrays = {"x": x.reshape(images, C, T), "weights": weights, "params": params}
    nc = bacc.Bacc("TRN2", target_bir_lowering=False, num_devices=1)
    args = [nc.dram_tensor(n, a.shape, F32, kind="ExternalInput").ap() for n, a in arrays.items()]
    state = nc.dram_tensor("state", (3 * images, C, T), F32, kind="ExternalOutput").ap()
    build(nc, *args, state, 2 * images, images)
    r = run(nc, [arrays], core_ids=[0])
    return r.results[0]["state"][2 * images:].reshape(x.shape)
```

```python
from contextlib import ExitStack

import concourse.bass as bass
import concourse.mybir as mybir

F32 = mybir.dt.float32
F32R = mybir.dt.float32r
ALU = mybir.AluOpType
ACT = mybir.ActivationFunctionType
AX = mybir.AxisListType

C, T = 512, 1024
HEADS, D = 8, 64
P = 128
KT = C // P
JT = T // P
NH = 512
HALVES = T // NH
BANKS = 3
PAIRS = HEADS // 2
QUARTERS = 4
QP, QN = P // QUARTERS, T // QUARTERS
GROUP = C // 32
EPS = 1e-5
SCALE = 1.0 / 8.0

GAMMA, BETA = 0, 4
AHEAD = 11
OWN = 17
BV, BO = 9, 13

STACK = [0, 2, 0, 1, 0, 2, 0, 1]

QK1, QK2, QK3, QK0, WV0, WV1, WO0, WO1 = range(8)
CHUNKS = 8
SLOT = [0, 1, 2, 0, 1, 2, 0, 1]
CHUNK_ROW = {QK0: 0, QK1: 1, QK2: 2, QK3: 3, WV0: 4, WV1: 5, WO0: 6, WO1: 7}
QK_CHUNK = [QK0, QK1, QK2, QK3]
PRO_CHUNKS = [QK0, WV0, WV1]
PRO = len(PRO_CHUNKS)

DRAINED_BY = {"q": "dve", "k": "dve", "max": "dve", "mrow": "act", "den": "act", "rec": "act",
              "gm": "dve", "gv": "dve", "v": "act", "out": "dve"}


FOR_ACT, FOR_DVE = ("q", "k", "mrow", "den", "rec", "v"), ("max", "gm", "gv", "out")


def qk_items(pair):
    return [(kind, pair, n) for kind in "qk" for n in range(HALVES)]


def max_items(head):
    return [("max", head, i) for i in range(JT * HALVES)]


STATS_AT = {(4, 0): 0, (4, 2): 1, (5, 6): 2, (6, 0): 3}
GROUP_AT = {(4, 1): [("gm", 0)], (4, 2): [("gv", 0)], (4, 3): [("gm", 1)], (4, 4): [("gv", 1)],
            (5, 7): [("gm", 2)], (6, 1): [("gv", 2), ("gm", 3)], (6, 2): [("gv", 3)]}
GAIN_AT = {(5, 0): 0, (5, 1): 1, (6, 3): 2, (6, 4): 3}
APPLY_AT = {(5, 2): 0, (5, 3): 1, (6, 4): 2, (6, 5): 3}
RSTD_AT = {(4, 2): [0], (4, 4): [1], (6, 1): [2], (6, 2): [3]}
H_LOW_AT = {(5, 1): 0, (5, 2): 1, (6, 2): 2, (6, 3): 3}

ADDED = {"dve": [1], "pool": [2, 3, 4, 5, 6, 7]}


def sum_of(tile):
    if tile == 0:
        return "dve", 0
    who = "dve" if tile in ADDED["dve"] else "pool"
    return who, ADDED[who].index(tile)


SPLIT_AT = {(0, 3): QK1, (1, 3): QK2, (3, 3): QK3, (3, 5): QK0, (4, 5): WV0, (7, 3): WV1, (7, 5): WO0}
SPLIT_AT_LAST = {(0, 3): QK1, (1, 3): QK2, (3, 3): QK3, (4, 3): WO0, (6, 3): WO1}


EVEN_STEPS = ["G,M,M,M", "G,M,M,M", "G,M,D,M", "G,M,M,M", "G,M,B,M", "G,R,M,M", "G,M,,", "G,,R,"]
ODD_STEPS = [",,Q,Q", ",D,K,BK", "G,,M,M", "G,M,M,M", "G,M,M,M", "M,M,R,M", "M,M,M,M", "GM,,,R"]
PIECES = 2
RECIP_AT = ({(3, 1): [0], (3, 2): [1]}, {(1, 0): [0, 1]})
NORMALIZE_AT = (6, 2)
ADD_AT = ({0: (2, 1)}, {0: (1, 1)})


def unit_slots(last):
    heads = []
    for h in range(HEADS):
        queues = {"D": [("den", h - 1, 0)] if h else [],
                  "B": [("rec", h - 1, 0)] if h else [],
                  "Q": [("q", (h + 1) // 2, n) for n in range(HALVES)],
                  "K": [("k", (h + 1) // 2, n) for n in range(HALVES)],
                  "M": max_items(h + 1),
                  "R": [("mrow", h + 1, n) for n in range(HALVES)]}
        heads.append([])
        for j, step in enumerate(ODD_STEPS[:] if h % 2 else EVEN_STEPS):
            slots = []
            for slot in step.split(","):
                items = []
                for kind in slot:
                    if kind == "G":
                        items += [] if last else [(g, kt, 0) for g, kt in GROUP_AT.get((h, j), [])]
                    elif kind in "DB":
                        items += queues[kind]
                    elif not (last and h == HEADS - 1):
                        items.append(queues[kind].pop(0))
                slots.append(items)
            heads[-1].append(slots)
        if not (last and h == HEADS - 1):
            assert not queues["M"] and not queues["R"]
    return heads


def unit_steps(last):
    return [[[i for slot in step for i in slot] for step in head] for head in unit_slots(last)]


def unit_tail(last):
    tail = [("v", t, 0) for t in range(JT)] if not last else []
    tail.insert(min(len(tail), 1), ("den", HEADS - 1, 0))
    tail.insert(min(len(tail), 4), ("rec", HEADS - 1, 0))
    return tail + [("out", m, n) for m in range(KT) for n in range(HALVES)]


def unit_items(last):
    return [i for row in unit_steps(last) for step in row for i in step] + unit_tail(last)


def prologue_items():
    items = []
    for kt in range(KT):
        items += [("gm", kt, 0), ("gv", kt, 0)]
    items += qk_items(0) + [("v", t, 0) for t in range(JT)] + max_items(0) + [("mrow", 0, n) for n in range(HALVES)]
    return items


def drained(items, who):
    return sum(DRAINED_BY[k] == who for k, _, _ in items)


def per_unit(items, kinds):
    return sum(k in kinds for k, _, _ in items)


class Count:

    def __init__(self, first, each):
        self.first, self.each = first, each

    def after(self, u, n):
        return u * self.each + (self.first + n)


def build(nc, x, weights, params, state, units, images):
    loop_items, pro_items = unit_items(False), prologue_items()

    DRAINED = {who: Count(drained(pro_items, who), drained(loop_items, who)) for who in ("dve", "act")}
    FILLED = {who: Count(per_unit(pro_items, kinds), per_unit(loop_items, kinds))
              for who, kinds in (("act", FOR_ACT), ("dve", FOR_DVE))}
    QKS = Count(4, 16)
    HIS = Count(8, 32)
    STEPS = Count(0, HEADS * JT)
    HALF_STEPS = Count(0, HEADS * JT * HALVES)
    ADDS = {who: Count(0, len(tiles) * HEADS) for who, tiles in ADDED.items()}
    HEADC = Count(0, HEADS)
    RECIPS = Count(0, PIECES * HEADS)
    PAIRC = Count(0, PAIRS)
    MAXC = Count(2, 2 * HEADS)
    MROWS = Count(2, 2 * HEADS)
    CHUNKC = Count(PRO, CHUNKS)
    GN = Count(KT, KT)
    RESIDS = [Count(0, 16 * len(range(b, KT, 3))) for b in range(3)]
    STORES = [Count(16 * len(range(b, images, 3)), RESIDS[b].each) for b in range(3)]
    assert images >= 3

    ctx = ExitStack()

    def sb(name, shape, dt=F32):
        return ctx.enter_context(nc.sbuf_tensor(name, shape, dt))

    def pb(name, shape):
        return ctx.enter_context(nc.psum_tensor(name, shape, F32))

    def sem(name):
        return ctx.enter_context(nc.semaphore(name))

    with ctx:
        x_tile = [sb(f"x_tile{i}", [P, T]) for i in range(2)]
        h_hi = sb("h_hi", [P, KT, T], F32R)
        h_lo = sb("h_lo", [P, KT, T], F32R)
        v_sb = sb("v_sb", [P, JT, C])
        w_stage = [sb(f"w_stage{i}", [P, 1024]) for i in range(2)]
        w_hi = sb("w_hi", [P, 3, 1024], F32R)
        w_lo = sb("w_lo", [P, 3, 1024], F32R)
        q_hh = [sb(f"q_hh{i}", [P, T], F32R) for i in range(3)]
        q_lm = [sb(f"q_lm{i}", [D + 1, T], F32R) for i in range(3)]
        k_hl = [sb(f"k_hl{i}", [P, T], F32R) for i in range(3)]
        k_h1 = [sb(f"k_h1{i}", [D + 1, T], F32R) for i in range(3)]
        probs = [sb(f"probs{i}", [P, T]) for i in range(4)]
        sum_dve = sb("sum_dve", [P, T])
        sum_pool = sb("sum_pool", [P, T])
        dens = sb("dens", [P, NH])
        o_nat = sb("o_nat", [P, T])
        o_hi = sb("o_hi", [P, PAIRS, T], F32R)
        o_lo = sb("o_lo", [P, PAIRS, T], F32R)
        resid = [*x_tile, sb("resid", [P, T])]
        ahead = sb("ahead", [P, AHEAD])
        own = sb("own", [P, OWN])
        ident = sb("ident", [P, P])
        ident_r = sb("ident_r", [P, P], F32R)
        group_avg = sb("group_avg", [P, P])
        ones = sb("ones", [P, QP])
        mx = sb("mx", [P, JT, HALVES])
        mcol = sb("mcol", [P, JT], F32R)
        stats = sb("stats", [P, HALVES, 6])
        meanvar = sb("meanvar", [P, 2])
        gmean = [sb(f"gmean{i}", [P, 1]) for i in range(2)]
        spread_sq = sb("spread_sq", [P, 1])
        veps = [sb(f"veps{i}", [P, 1]) for i in range(2)]
        rstd = [sb(f"rstd{i}", [P, 1]) for i in range(2)]
        gain = [sb(f"gain{i}", [P, 1]) for i in range(2)]
        shift = [sb(f"shift{i}", [P, 1]) for i in range(2)]
        minus_half = sb("minus_half", [P, 1])
        pace = sb("pace", [P, 1])

        s_ps = [pb(f"s_ps{i}", [P, NH]) for i in range(BANKS)]
        work = [pb(f"work{i}", [P, NH]) for i in range(BANKS)]
        o_ps = [pb(f"o_ps{i}", [P, NH]) for i in range(2)]

        x_loaded = [sem(f"x_loaded{i}") for i in range(2)]
        w_loaded = [sem(f"w_loaded{i}") for i in range(2)]
        resid_loaded = [sem(f"resid_loaded{i}") for i in range(3)]
        ahead_loaded = sem("ahead_loaded")
        own_loaded = sem("own_loaded")
        stored = [sem(f"stored{i}") for i in range(3)]
        filled = {"act": sem("filled_for_act"), "dve": sem("filled_for_dve")}
        scores_made = sem("scores_made")
        values_used = sem("values_used")
        act_drained = sem("act_drained")
        hi_made = sem("hi_made")
        hi_copied = sem("hi_copied")
        w_hi_made = sem("w_hi_made")
        applied = sem("applied")
        exps_done = sem("exps_done")
        o_hi_made = sem("o_hi_made")
        dve_drained = sem("dve_drained")
        shifts_made = sem("shifts_made")
        consts_dve = sem("consts_dve")
        adds_dve = sem("adds_dve")
        maxima_made = sem("maxima_made")
        recips_made = sem("recips_made")
        o_normed = sem("o_normed")
        mx_parts = sem("mx_parts")
        stats_parts = sem("stats_parts")
        spread_steps = sem("spread_steps")
        gains_made = sem("gains_made")
        stats_made = sem("stats_made")
        spread_made = sem("spread_made")
        consts_pool = sem("consts_pool")
        masks = sem("masks")
        adds_pool = sem("adds_pool")
        w_split = sem("w_split")
        h_made = sem("h_made")
        o_lo_made = sem("o_lo_made")
        rstd_made = sem("rstd_made")

        block = ctx.enter_context(nc.Block())

        def w_tiles(chunk):
            n = 2 if chunk in (WV0, WV1) else 4
            return (w_hi[:, SLOT[chunk], :].rearrange("p (k c) -> p k c", k=n),
                    w_lo[:, SLOT[chunk], :].rearrange("p (k c) -> p k c", k=n))

        def qk_params(kind, pair):
            if pair == 0:
                return ahead, 8 + (kind == "k")
            return own, 3 * (pair - 1) + (kind == "k")

        def chunk_place(i, last):
            return QK3 + 1 + i - WO0 if last and i >= WO0 else i

        def over_units(eng, body):
            if units > 1:
                with eng.Fori(0, units - 1) as u:
                    body(u, False)
            body(units - 1, True)

        @block.sync
        def _(sp):
            def load_chunk(n, nth, row, first):
                if not first:
                    sp.wait_ge(w_split, nth)
                sp.dma_start(w_stage[n][:, :], row).then_inc(w_loaded[n], 16)

            sp.dma_start(ahead[:, :], params[0, :, 0:AHEAD]).then_inc(ahead_loaded, 16)
            for kt in range(2):
                sp.dma_start(x_tile[kt][:, :], x[0, kt * P:(kt + 1) * P, :]).then_inc(x_loaded[kt], 16)
            for n in range(2):
                load_chunk((n + 1) % 2, n, weights[0, CHUNK_ROW[PRO_CHUNKS[n]]], True)
            for kt in range(2, KT):
                sp.wait_ge(h_made, kt - 1)
                sp.dma_start(x_tile[kt % 2][:, :], x[0, kt * P:(kt + 1) * P, :]).then_inc(x_loaded[kt % 2], 16)
            load_chunk(1, 1, weights[0, CHUNK_ROW[PRO_CHUNKS[2]]], False)
            for b in range(images):
                sp.dma_start(state[b], x[b]).then_inc(stored[b % 3], 16)

            def unit(u, last):
                def held(value):
                    return value if isinstance(value, int) else sp.snap(value)

                layer, here, made = held(u // images), held(u + 0), held(u + images)
                if not last:
                    after, nxt = held((u + 1) // images), held(u + 1)
                items = unit_items(last)
                splits = [held(CHUNKC.after(u, i - 1)) for i in range(CHUNKS if not last else QK3 + 3)]
                gn_done = {k: held(GN.after(u, k)) for k in (0, 1, 2, KT)} if not last else {}
                outs = [held(DRAINED["dve"].after(u, drained(items[:items.index(("out", m, HALVES - 1)) + 1], "dve")))
                        for m in range(KT)]
                stores = [held(STORES[m % 3].after(u, 16 * (m // 3 + 1))) for m in range(KT if last else KT - 3)]
                earlier = [held(STORES[b].after(u, 0)) for b in range(3)]

                def chunk(i):
                    of = after if i in (QK0, WV0, WV1) else layer
                    load_chunk(i % 2, splits[i], weights[of, CHUNK_ROW[i]], False)

                def x_load(kt):
                    sp.dma_start(x_tile[kt % 2][:, :], state[nxt, kt * P:(kt + 1) * P, :]).then_inc(x_loaded[kt % 2], 16)

                def rows(m):
                    return slice(m * P, (m + 1) * P)

                chunk(QK1)
                sp.dma_start(own[:, :], params[layer, :, AHEAD:]).then_inc(own_loaded, 16)
                chunk(QK2)
                chunk(QK3)
                if not last:
                    chunk(QK0)
                    sp.wait_ge(stored[0], earlier[0])
                    sp.wait_ge(stored[1], earlier[1])
                    sp.dma_start(ahead[:, :], params[after, :, 0:AHEAD]).then_inc(ahead_loaded, 16)
                    sp.wait_ge(stored[2], earlier[2])
                    sp.wait_ge(h_made, gn_done[0])
                    x_load(0)
                    x_load(1)
                    chunk(WV0)
                    chunk(WV1)
                    chunk(WO0)
                    sp.wait_ge(h_made, gn_done[1])
                    x_load(2)
                    sp.wait_ge(h_made, gn_done[2])
                    x_load(3)
                    chunk(WO1)
                    sp.wait_ge(h_made, gn_done[KT])
                else:
                    for i in (WO0, WO1):
                        place = chunk_place(i, last)
                        load_chunk(place % 2, splits[place], weights[layer, CHUNK_ROW[i]], False)
                    for b in range(3):
                        sp.wait_ge(stored[b], earlier[b])

                def load(m):
                    if m >= 3:
                        sp.wait_ge(stored[m % 3], stores[m - 3])
                    sp.dma_start(resid[m % 3][:, :], state[here, rows(m), :]).then_inc(resid_loaded[m % 3], 16)

                for m in range(3):
                    load(m)
                for m in range(KT):
                    if m == 1:
                        load(3)
                    sp.wait_ge(dve_drained, outs[m])
                    sp.dma_start(state[made, rows(m), :], resid[m % 3][:, :]).then_inc(stored[m % 3], 16)
                if last:
                    for m in range(1, KT):
                        sp.wait_ge(stored[m % 3], stores[m])

            over_units(sp, unit)

        @block.gpsimd
        def _(pool):
            nc.gpsimd.memset(ident[:, :], 0.0).then_inc(masks, 1)
            nc.gpsimd.memset(group_avg[:, :], 1.0 / GROUP).then_inc(masks, 1)
            nc.gpsimd.memset(ones[:, :], 1.0).then_inc(consts_pool, 1)
            nc.gpsimd.memset(minus_half[:, :], -0.5).then_inc(consts_pool, 1)
            pool.wait_ge(masks, 2)
            nc.gpsimd.affine_select(out=ident[:, :], in_=ident[:, :], compare_op=ALU.not_equal, fill=1.0,
                                    base=0, pattern=[[-1, P]], channel_multiplier=1).then_inc(consts_pool, 1)
            by_group = group_avg[:, :].rearrange("p (g c) -> p g c", c=GROUP)
            nc.gpsimd.affine_select(out=by_group, in_=by_group, compare_op=ALU.is_ge, fill=0.0, base=0,
                                    pattern=[[-GROUP, P // GROUP], [0, GROUP]], channel_multiplier=1).then_inc(masks, 1)
            pool.wait_ge(masks, 3)
            nc.gpsimd.affine_select(out=by_group, in_=by_group, compare_op=ALU.is_ge, fill=0.0, base=GROUP - 1,
                                    pattern=[[GROUP, P // GROUP], [0, GROUP]], channel_multiplier=-1).then_inc(consts_pool, 1)
            pool.wait_ge(consts_pool, 4)

            def w_low(chunk, stage, nth):
                pool.wait_ge(w_hi_made, nth + 1)
                nc.gpsimd.tensor_tensor(w_lo[:, SLOT[chunk], :], w_stage[stage][:, :],
                                        w_hi[:, SLOT[chunk], :].bitcast(F32), ALU.subtract).then_inc(w_split, 1)

            def h_low(kt, nth):
                pool.wait_ge(applied, nth + 1)
                nc.gpsimd.tensor_tensor(h_lo[:, kt, :], x_tile[kt % 2][:, :], h_hi[:, kt, :].bitcast(F32),
                                        ALU.subtract).then_inc(h_made, 1)

            def rstd_of(kt, drained_to):
                pool.wait_ge(dve_drained, drained_to)
                nc.gpsimd.tensor_tensor(rstd[kt % 2][:, :], veps[kt % 2][:, :], minus_half[:, :], ALU.pow).then_inc(rstd_made, 1)

            for kt in range(KT):
                rstd_of(kt, drained(pro_items[:pro_items.index(("gv", kt, 0)) + 1], "dve"))
                if kt < 2:
                    w_low(PRO_CHUNKS[kt], (kt + 1) % 2, kt)
                h_low(kt, kt)
            w_low(WV1, 1, 2)

            def unit(u, last):
                items = unit_items(last)

                splits = SPLIT_AT_LAST if last else SPLIT_AT

                def w_low_here(i):
                    place = chunk_place(i, last)
                    w_low(i, place % 2, CHUNKC.after(u, place))

                def o_low(pair):
                    pool.wait_ge(o_hi_made, PAIRC.after(u, pair + 1))
                    nc.gpsimd.tensor_tensor(o_lo[:, pair, :], o_nat[:, :], o_hi[:, pair, :].bitcast(F32),
                                            ALU.subtract).then_inc(o_lo_made, 1)

                def add(h, k):
                    j = ADDED["pool"][k]
                    if k == 0:
                        pool.wait_ge(adds_dve, ADDS["dve"].after(u, len(ADDED["dve"]) * (h + 1)))
                    if k == 0 and h > 0:
                        upto = items[:items.index(("den", h - 1, 0)) + 1]
                        pool.wait_ge(filled["act"], FILLED["act"].after(u, per_unit(upto, FOR_ACT)))
                    if k > 0:
                        pool.wait_ge(adds_pool, ADDS["pool"].after(u, len(ADDED["pool"]) * h + k))
                    pool.wait_ge(exps_done, HALF_STEPS.after(u, (h * JT + j + 1) * HALVES))
                    first = sum_dve if k == 0 else sum_pool
                    nc.gpsimd.tensor_tensor(sum_pool[:, :], first[:, :], probs[j % 4][:, :], ALU.add).then_inc(adds_pool, 1)

                for h in range(HEADS):
                    if h in (3, 5, 7):
                        o_low(h // 2 - 1)
                    for k in range(len(ADDED["pool"])):
                        if not last:
                            for kt in RSTD_AT.get((h, k), []):
                                upto = items[:items.index(("gv", kt, 0)) + 1]
                                rstd_of(kt, DRAINED["dve"].after(u, drained(upto, "dve")))
                            if (h, k) in H_LOW_AT:
                                kt = H_LOW_AT[h, k]
                                h_low(kt, GN.after(u, kt))
                        if (h, ADDED["pool"][k]) in splits:
                            w_low_here(splits[h, ADDED["pool"][k]])
                        add(h, k)
                o_low(PAIRS - 1)
                if not last:
                    w_low_here(WO1)

            over_units(pool, unit)

        @block.scalar
        def _(act):
            def filled_of(kinds_items, item):
                upto = kinds_items[:kinds_items.index(item) + 1]
                return per_unit(upto, FOR_ACT)

            def qk_hi(item, bank, heads, col, par, his, nth):
                kind, _, n = item
                for half, s in enumerate(heads):
                    rows = slice(half * D, (half + 1) * D)
                    src, bias = work[bank][rows, :], par[rows, col:col + 1]
                    cols = slice(n * NH, (n + 1) * NH)
                    out = q_hh[s][rows, cols] if kind == "q" else k_hl[s][0:D, cols]
                    nc.scalar.activation(out, src, ACT.Identity, bias=bias).then_inc(hi_made, 1)
                for half, s in enumerate(heads):
                    act.wait_ge(hi_made, his(nth - 1 + half))
                    if kind == "q":
                        rows, other = [slice(k * D, (k + 1) * D) for k in (half, 1 - half)]
                        done = nc.scalar.copy(q_hh[s][other, cols], q_hh[s][rows, cols])
                    else:
                        done = nc.scalar.copy(k_h1[s][0:D, cols], k_hl[s][0:D, cols])
                done.then_inc(hi_copied, 1)

            def mrow(item, bank, s):
                n = item[2]
                nc.scalar.activation(q_lm[s][D:D + 1, n * NH:(n + 1) * NH], work[bank][0:1, :], ACT.Copy,
                                     scale=-1.0).then_inc(act_drained, 1)

            def take(items, item, at, his, normed=None):
                kind, a, n = item
                bank = items.index(item) % BANKS
                act.wait_ge(filled["act"], at(filled_of(items, item)))
                if kind in "qk":
                    pair = a % PAIRS
                    par, col = qk_params(kind, pair)
                    nth = 2 * per_unit(items[:items.index(item)], "qk") + 2
                    qk_hi(item, bank, (STACK[2 * pair], STACK[2 * pair + 1]), col, par, his, nth)
                elif kind == "mrow":
                    mrow(item, bank, STACK[a % HEADS])
                elif kind == "den":
                    if a > 0:
                        act.wait_ge(o_normed, normed(a))
                    nc.scalar.copy(dens[:, 0:QN], work[bank][:, 0:QN]).then_inc(act_drained, 1)
                elif kind == "rec":
                    nc.scalar.copy(dens[:, :], work[bank][:, :]).then_inc(act_drained, 1)
                else:
                    nc.scalar.copy(v_sb[:, a, :], work[bank][:, :]).then_inc(act_drained, 1)

            def w_high(chunk, stage, loads):
                act.wait_ge(w_loaded[stage], loads)
                nc.scalar.copy(w_hi[:, SLOT[chunk], :], w_stage[stage][:, :]).then_inc(w_hi_made, 1)

            def gn_apply(kt, nth):
                act.wait_ge(shifts_made, nth + 1)
                g, b = gain[kt % 2][:, :], shift[kt % 2][:, :]
                nc.scalar.activation(h_hi[:, kt, :], x_tile[kt % 2][:, :], ACT.Identity, bias=b, scale=g)
                nc.scalar.activation(x_tile[kt % 2][:, :], x_tile[kt % 2][:, :], ACT.Identity, bias=b,
                                     scale=g).then_inc(applied, 1)

            act.wait_ge(ahead_loaded, 16)
            w_high(QK0, 1, 16)
            w_high(WV0, 0, 16)
            for kt in range(KT):
                gn_apply(kt, kt)
            act.wait_ge(w_split, 1)
            w_high(WV1, 1, 32)
            for item in pro_items:
                if item[0] in FOR_ACT:
                    take(pro_items, item, lambda n: n, lambda n: n)

            def unit(u, last):
                items, slots = unit_items(last), unit_slots(last)
                splits = SPLIT_AT_LAST if last else SPLIT_AT

                def at(n):
                    return FILLED["act"].after(u, n)

                def normed(n):
                    return HEADC.after(u, n)

                def his(n):
                    return HIS.after(u, n)

                def o_high(pair):
                    act.wait_ge(o_normed, HEADC.after(u, 2 * pair + 2))
                    bias = own[:, BV + pair:BV + pair + 1]
                    nc.scalar.activation(o_hi[:, pair, :], o_nat[:, :], ACT.Identity, bias=bias)
                    nc.scalar.activation(o_nat[:, :], o_nat[:, :], ACT.Identity, bias=bias).then_inc(o_hi_made, 1)

                def w_high_here(i):
                    place = chunk_place(i, last)
                    if i in (QK1, QK2, QK3):
                        act.wait_ge(filled["act"], FILLED["act"].after(u, 0))
                        act.wait_ge(filled["dve"], FILLED["dve"].after(u, 0))
                    else:
                        user = {QK0: ("k", 1, 1), WV0: ("k", 2, 1), WV1: ("k", 3, 1),
                                WO0: ("k", 1 if last else 4, 1), WO1: ("k", 2, 1) if last else ("v", JT - 1, 0)}[i]
                        upto = items[:items.index(user) + 1]
                        act.wait_ge(filled["act"], FILLED["act"].after(u, per_unit(upto, FOR_ACT)))
                    w_high(i, place % 2, Count(16 * (1 + place % 2), 64).after(u, 16 * (place // 2 + 1)))

                def exp(h, j):
                    if h > 0 or j >= 4:
                        act.wait_ge(values_used, STEPS.after(u, h * JT + j - 3))
                        who, k = sum_of((j - 4) % JT)
                        head = h if j >= 4 else h - 1
                        act.wait_ge(adds_dve if who == "dve" else adds_pool,
                                    ADDS[who].after(u, len(ADDED[who]) * head + k + 1))
                    for n in range(HALVES):
                        g = (h * JT + j) * HALVES + n
                        act.wait_ge(scores_made, HALF_STEPS.after(u, g + 1))
                        nc.scalar.activation(probs[j % 4][:, n * NH:(n + 1) * NH], s_ps[g % BANKS][:, :], ACT.Exp,
                                             scale=SCALE).then_inc(exps_done, 1)

                for h in range(HEADS):
                    if h == 1:
                        act.wait_ge(own_loaded, Count(0, 16).after(u, 16))
                    if h == HEADS - 1 and not last:
                        act.wait_ge(ahead_loaded, Count(16, 16).after(u, 16))
                    for j in range(JT):
                        before, between, behind, end = slots[h][j]
                        for item in before + between + behind:
                            if item[0] in FOR_ACT and (item not in behind or item[0] == "mrow"):
                                take(items, item, at, his, normed)
                        exp(h, j)
                        for item in behind + end:
                            if item[0] in FOR_ACT and (item not in behind or item[0] != "mrow"):
                                take(items, item, at, his, normed)
                        if j == JT - 1 and h in (2, 4, 6):
                            o_high(h // 2 - 1)
                        if (h, j + 1) in splits:
                            w_high_here(splits[h, j + 1])
                        if not last and (h, j) in APPLY_AT:
                            kt = APPLY_AT[h, j]
                            gn_apply(kt, GN.after(u, kt))
                for item in unit_tail(last):
                    if item[0] in FOR_ACT:
                        take(items, item, at, his, normed)
                    if item == ("v", 4, 0):
                        o_high(PAIRS - 1)
                if last:
                    o_high(PAIRS - 1)
                else:
                    w_high_here(WO1)

            over_units(act, unit)

        @block.vector
        def _(dve):
            v = nc.vector

            def filled_of(items, item):
                upto = items[:items.index(item) + 1]
                return per_unit(upto, FOR_DVE)

            def qks_of(items, item):
                upto = items[:items.index(item) + 1]
                return per_unit(upto, ("q", "k"))

            def qk_lo(item, bank, heads, col, par, his):
                kind, _, n = item
                cols = slice(n * NH, (n + 1) * NH)
                for half, s in enumerate(heads):
                    rows = slice(half * D, (half + 1) * D)
                    src = work[bank][rows, :]
                    if kind == "q":
                        hi, bias, out = q_hh[s][rows, cols], par[rows, col:col + 1], q_lm[s][0:D, cols]
                    else:
                        hi, bias, out = k_hl[s][0:D, cols], par[0:D, col + half:col + half + 1], k_hl[s][D:P, cols]
                    dve.wait_ge(hi_made, his[half])
                    done = v.scalar_tensor_tensor(out=out, in0=src, scalar=bias, in1=hi.bitcast(F32),
                                                  op0=ALU.add, op1=ALU.subtract)
                done.then_inc(dve_drained, 1)

            def gn_stats(kt, nth_load, nth):
                dve.wait_ge(x_loaded[kt % 2], nth_load)
                for n in range(HALVES):
                    v.bn_stats(stats[:, n, :], x_tile[kt % 2][:, n * NH:(n + 1) * NH]).then_inc(stats_parts, 1)
                dve.wait_ge(stats_parts, 2 * nth + 2)
                v.memset(pace[:, :], 0.0)
                v.bn_aggr(meanvar[:, :], stats[:, :, :]).then_inc(stats_made, 1)

            def gn_mean(kt, bank, nth):
                v.tensor_tensor(spread_sq[:, :], meanvar[:, 0:1], work[bank][:, 0:1], ALU.subtract).then_inc(spread_steps, 1)
                v.tensor_copy(gmean[kt % 2][:, :], work[bank][:, 0:1]).then_inc(dve_drained, 1)
                dve.wait_ge(spread_steps, 2 * nth + 1)
                v.tensor_tensor(spread_sq[:, :], spread_sq[:, :], spread_sq[:, :], ALU.mult).then_inc(spread_steps, 1)
                dve.wait_ge(spread_steps, 2 * nth + 2)
                v.tensor_tensor(spread_sq[:, :], spread_sq[:, :], meanvar[:, 1:2], ALU.add).then_inc(spread_made, 1)

            def gn_var(kt, bank):
                done = v.tensor_scalar(veps[kt % 2][:, :], work[bank][:, 0:1], EPS, None, ALU.add)
                done.then_inc(dve_drained, 1)

            def gn_gain(kt, nth):
                dve.wait_ge(rstd_made, nth + 1)
                v.tensor_tensor(gain[kt % 2][:, :], rstd[kt % 2][:, :], ahead[:, GAMMA + kt:GAMMA + kt + 1],
                                ALU.mult).then_inc(gains_made, 1)
                dve.wait_ge(gains_made, nth + 1)
                v.scalar_tensor_tensor(out=shift[kt % 2][:, :], in0=gmean[kt % 2][:, :], scalar=gain[kt % 2][:, :],
                                       in1=ahead[:, BETA + kt:BETA + kt + 1], op0=ALU.mult, op1=ALU.subtract,
                                       reverse1=True).then_inc(shifts_made, 1)

            def maximum(item, bank, nth_head):
                t, n = divmod(item[2], HALVES)
                ins = v.reduce_max(mx[:, t, n:n + 1], work[bank][:, :], axis=AX.X)
                ins.then_inc(dve_drained, 1)

            def maxima(half, drained_to):
                dve.wait_ge(dve_drained, drained_to)
                rows = slice(half * JT // 2, (half + 1) * JT // 2)
                v.tensor_tensor(mcol[:, rows], mx[:, rows, 0], mx[:, rows, 1], ALU.max).then_inc(maxima_made, 1)

            def take(items, item, at, u):
                kind, a, n = item
                bank = items.index(item) % BANKS
                upto = drained(items[:items.index(item) + 1], "dve")
                if kind in "qk":
                    pair = a % PAIRS
                    par, col = qk_params(kind, pair)
                    his = [at("hi", 2 * qks_of(items, item) - 1 + half) for half in range(2)]
                    qk_lo(item, bank, (STACK[2 * pair], STACK[2 * pair + 1]), col, par, his)
                    return
                dve.wait_ge(filled["dve"], at("filled", filled_of(items, item)))
                if kind == "max":
                    maximum(item, bank, None)
                    if (n + 1) % JT == 0:
                        maxima(n // JT, at("drained", upto))
                elif kind == "gm":
                    gn_mean(a, bank, at("gn", a))
                elif kind == "gv":
                    gn_var(a, bank)
                elif kind == "out":
                    tile, cols = resid[a % 3], slice(n * NH, (n + 1) * NH)
                    if n == 0:
                        dve.wait_ge(resid_loaded[a % 3], RESIDS[a % 3].after(u, 16 * (a // 3 + 1)))
                    done = v.scalar_tensor_tensor(out=tile[:, cols], in0=work[bank][:, :],
                                                  scalar=own[:, BO + a:BO + a + 1], in1=tile[:, cols],
                                                  op0=ALU.add, op1=ALU.add)
                    done.then_inc(dve_drained, 1)

            def before_loop(what, n):
                return n

            for s in range(3):
                v.memset(k_h1[s][D:D + 1, :].bitcast(F32), 1.0).then_inc(consts_dve, 1)
            dve.wait_ge(consts_pool, 4)
            v.tensor_copy(ident_r[:, :], ident[:, :]).then_inc(consts_dve, 1)
            dve.wait_ge(ahead_loaded, 16)
            for kt in range(KT):
                gn_stats(kt, 16 * (kt // 2 + 1), kt)
                take(pro_items, ("gm", kt, 0), before_loop, 0)
                take(pro_items, ("gv", kt, 0), before_loop, 0)
                gn_gain(kt, kt)
            for item in pro_items:
                if item[0] in ("q", "k", "max"):
                    take(pro_items, item, before_loop, 0)

            def unit(u, last):
                items, steps = unit_items(last), unit_steps(last)

                def at(what, n):
                    return {"hi": HIS, "filled": FILLED["dve"], "drained": DRAINED["dve"], "gn": GN}[what].after(u, n)

                def add(h, k):
                    j = ADDED["dve"][k]
                    if h > 0:
                        dve.wait_ge(adds_pool, ADDS["pool"].after(u, len(ADDED["pool"]) * (h - 1) + 1))
                    dve.wait_ge(exps_done, HALF_STEPS.after(u, (h * JT + j + 1) * HALVES))
                    v.tensor_tensor(sum_dve[:, :], probs[0][:, :], probs[j % 4][:, :], ALU.add).then_inc(adds_dve, 1)

                def reciprocal(h, piece):
                    if piece == 0:
                        upto = items[:items.index(("den", h, 0)) + 1]
                        dve.wait_ge(act_drained, DRAINED["act"].after(u, drained(upto, "act")))
                    cols = slice(piece * P, (piece + 1) * P)
                    v.reciprocal(dens[:, cols], dens[:, cols]).then_inc(recips_made, 1)

                def normalize(h):
                    upto = items[:items.index(("rec", h, 0)) + 1]
                    dve.wait_ge(act_drained, DRAINED["act"].after(u, drained(upto, "act")))
                    if h >= 2 and h % 2 == 0:
                        dve.wait_ge(o_lo_made, PAIRC.after(u, h // 2))
                    for half in range(HALVES):
                        rows = slice(half * D, (half + 1) * D)
                        done = v.tensor_tensor(o_nat[h % 2 * D:(h % 2 + 1) * D, half * NH:(half + 1) * NH],
                                               o_ps[h % 2][rows, :], dens[rows, :], ALU.mult)
                    done.then_inc(o_normed, 1)

                for h in range(HEADS):
                    if h == 1:
                        dve.wait_ge(own_loaded, Count(0, 16).after(u, 16))
                    if h == 5 and not last:
                        dve.wait_ge(ahead_loaded, Count(16, 16).after(u, 16))
                    for j in range(JT):
                        if not last and (h, j) in STATS_AT:
                            kt = STATS_AT[h, j]
                            gn_stats(kt, Count(32, 32).after(u, 16 * (kt // 2 + 1)), GN.after(u, kt))
                        mine = [i for i in steps[h][j] if DRAINED_BY[i[0]] == "dve"]
                        adds = [k for k, (step, _) in ADD_AT[h % 2].items() if step == j]
                        for n, item in enumerate(mine):
                            for k in adds:
                                if ADD_AT[h % 2][k][1] == n:
                                    add(h, k)
                            for piece in RECIP_AT[h % 2].get((j, n), []) if h > 0 else []:
                                reciprocal(h - 1, piece)
                            take(items, item, at, u)
                        if not mine:
                            for k in adds:
                                add(h, k)
                        if not last and (h, j) in GAIN_AT:
                            kt = GAIN_AT[h, j]
                            gn_gain(kt, GN.after(u, kt))
                        if last and h == HEADS - 1 and j == 1:
                            for piece in range(PIECES):
                                reciprocal(h - 1, piece)
                        if h > 0 and j == NORMALIZE_AT[h % 2]:
                            normalize(h - 1)
                for piece in range(PIECES):
                    reciprocal(HEADS - 1, piece)
                normalize(HEADS - 1)
                for item in unit_tail(last):
                    if item[0] == "out":
                        take(items, item, at, u)

            over_units(dve, unit)

        @block.tensor
        def _(pe):
            mm = nc.tensor.matmul

            def three(out, w, x, k, n, flip=False):
                (wh, wl), (xh, xl) = w, x
                pairs = [(xh, wh), (xh, wl), (xl, wh)] if flip else [(wh, xh), (wl, xh), (wh, xl)]
                for i, (a, b) in enumerate(pairs):
                    last = mm(out, a, b, start=(k == 0 and i == 0), stop=(k == n - 1 and i == 2))
                return last

            def fill(items, item, prior, u):
                kind, a, n = item
                pos = items.index(item)
                bank = work[pos % BANKS]
                if pos < BANKS:
                    for before in (loop_items, pro_items) if prior is not None else ():
                        at = max(i for i in range(len(before)) if i % BANKS == pos)
                        who = DRAINED_BY[before[at][0]]
                        pe.wait_ge(dve_drained if who == "dve" else act_drained, prior(who, -drained(before[at + 1:], who)))
                else:
                    who = DRAINED_BY[items[pos - BANKS][0]]
                    upto = drained(items[:pos - BANKS + 1], who)
                    pe.wait_ge(dve_drained if who == "dve" else act_drained, upto if prior is None else prior(who, upto))
                if kind in "qk":
                    wh, wl = w_tiles(QK_CHUNK[a % PAIRS])
                    cols = slice(0, P) if kind == "q" else slice(P, 2 * P)
                    for k in range(KT):
                        if kind == "q" and n == 0 and a in (0, PAIRS):
                            pe.wait_ge(h_made, k + 1 if prior is None else GN.after(u, k + 1))
                        last = three(bank[:, :], (wh[:, k, cols], wl[:, k, cols]),
                                     (h_hi[:, k, n * NH:(n + 1) * NH], h_lo[:, k, n * NH:(n + 1) * NH]), k, KT)
                    last.then_inc(filled["act"], 1)
                elif kind == "max":
                    s = STACK[a % HEADS]
                    t, half = divmod(n, HALVES)
                    mm(bank[:, :], q_hh[s][0:D, t * P:(t + 1) * P], k_hl[s][0:D, half * NH:(half + 1) * NH],
                       start=True, stop=True).then_inc(filled["dve"], 1)
                elif kind == "mrow":
                    for t in range(JT // HALVES):
                        last = mm(bank[0:1, t * P:(t + 1) * P], mcol[:, n * 4 + t:n * 4 + t + 1], ident_r[:, :],
                                  start=True, stop=True)
                    last.then_inc(filled["act"], 1)
                elif kind == "den":
                    for c in range(QUARTERS):
                        last = mm(bank[c * QP:(c + 1) * QP, 0:QN], ones[:, :], sum_pool[:, c * QN:(c + 1) * QN],
                                  start=True, stop=True)
                    last.then_inc(filled["act"], 1)
                elif kind == "rec":
                    for i in range(QUARTERS // HALVES):
                        for half in range(HALVES):
                            row = (half * QUARTERS // HALVES + i) * QP
                            last = mm(bank[half * D:(half + 1) * D, i * QN:(i + 1) * QN],
                                      ident[:, row:row + 1].to_broadcast([P, D]), dens[:, 0:QN], start=True, stop=True)
                    last.then_inc(filled["act"], 1)
                elif kind == "gm":
                    mm(bank[:, 0:1], group_avg[:, :], meanvar[:, 0:1], start=True, stop=True).then_inc(filled["dve"], 1)
                elif kind == "gv":
                    mm(bank[:, 0:1], group_avg[:, :], spread_sq[:, :], start=True, stop=True).then_inc(filled["dve"], 1)
                elif kind == "v":
                    for k in range(KT):
                        wh, wl = w_tiles(WV0 if k < 2 else WV1)
                        tok = slice(a * P, (a + 1) * P)
                        last = three(bank[:, :], (wh[:, k % 2, :], wl[:, k % 2, :]),
                                     (h_hi[:, k, tok], h_lo[:, k, tok]), k, KT, flip=True)
                    last.then_inc(filled["act"], 1)
                elif kind == "out":
                    wh, wl = w_tiles(WO0 if a < 2 else WO1)
                    cols = slice(a % 2 * P, (a % 2 + 1) * P)
                    for k in range(KT):
                        half = slice(n * NH, (n + 1) * NH)
                        last = three(bank[:, :], (wh[:, k, cols], wl[:, k, cols]), (o_hi[:, k, half], o_lo[:, k, half]), k, KT)
                    last.then_inc(filled["dve"], 1)

            pe.wait_ge(consts_pool, 4)
            pe.wait_ge(consts_dve, 4)
            for item in pro_items:
                kind, a, n = item
                if kind == "gm":
                    pe.wait_ge(stats_made, a + 1)
                elif kind == "gv":
                    pe.wait_ge(spread_made, a + 1)
                elif kind == "q" and n == 0:
                    pe.wait_ge(w_split, PRO)
                elif kind == "max" and n == 0:
                    pe.wait_ge(dve_drained, drained(pro_items[:pro_items.index(item)], "dve"))
                elif kind == "mrow":
                    pe.wait_ge(maxima_made, n + 1)
                fill(pro_items, item, None, 0)

            def unit(u, last):
                items, slots = unit_items(last), unit_slots(last)

                def prior(who, n):
                    return DRAINED[who].after(u, n)

                def scores(h, j, n):
                    g, s = (h * JT + j) * HALVES + n, STACK[h]
                    if h % 2 == 0 and j == 0 and n == 0:
                        pe.wait_ge(hi_copied, QKS.after(u, 4 * (h // 2)))
                    if g >= BANKS:
                        pe.wait_ge(exps_done, HALF_STEPS.after(u, g - BANKS + 1))
                    out, keys, half = s_ps[g % BANKS][:, :], slice(j * P, (j + 1) * P), slice(n * NH, (n + 1) * NH)
                    mm(out, k_hl[s][:, keys], q_hh[s][:, half], start=True, stop=False)
                    if j == 0:
                        upto = items[:items.index(("mrow", h, n)) + 1] if h > 0 else []
                        pe.wait_ge(act_drained, DRAINED["act"].after(u, drained(upto, "act")))
                    mm(out, k_h1[s][:, keys], q_lm[s][:, half], start=False, stop=True).then_inc(scores_made, 1)

                def values(h, j):
                    pe.wait_ge(exps_done, HALF_STEPS.after(u, (h * JT + j + 1) * HALVES))
                    if j == 0 and h >= 2:
                        pe.wait_ge(o_normed, HEADC.after(u, h - 1))
                    for half in range(HALVES):
                        done = mm(o_ps[h % 2][half * D:(half + 1) * D, :], v_sb[:, j, h * D:(h + 1) * D],
                                  probs[j % 4][:, half * NH:(half + 1) * NH], start=(j == 0), stop=(j == JT - 1))
                    done.then_inc(values_used, 1)

                def ready(item):
                    kind, a, n = item
                    if kind == "gm":
                        pe.wait_ge(stats_made, GN.after(u, a + 1))
                    elif kind == "gv":
                        pe.wait_ge(spread_made, GN.after(u, a + 1))
                    elif kind == "q" and n == 0:
                        chunk = QK_CHUNK[a % PAIRS]
                        pe.wait_ge(w_split, CHUNKC.after(u, chunk + 1))
                    elif kind == "max" and n == 0 and a % 2:
                        pe.wait_ge(hi_copied, QKS.after(u, 4 * (a // 2)))
                    elif kind == "max" and n < HALVES:
                        pe.wait_ge(hi_made, HIS.after(u, 2 * (4 * (a // 2 - 1) + HALVES + n + 1)))
                    elif kind == "mrow":
                        pe.wait_ge(maxima_made, MAXC.after(u, 2 * a - 1 + n))
                    elif kind == "den":
                        pe.wait_ge(adds_pool, ADDS["pool"].after(u, len(ADDED["pool"]) * (a + 1)))
                    elif kind == "rec":
                        pe.wait_ge(recips_made, RECIPS.after(u, PIECES * (a + 1)))
                    elif kind == "v" and a == 0:
                        pe.wait_ge(w_split, CHUNKC.after(u, WV1 + 1))
                    elif kind == "out" and n == 0 and a % 2 == 0:
                        if a == 0:
                            pe.wait_ge(o_lo_made, PAIRC.after(u, PAIRS))
                        pe.wait_ge(w_split, CHUNKC.after(u, chunk_place(WO0 if a == 0 else WO1, last) + 1))

                def make(item):
                    ready(item)
                    fill(items, item, prior, u)

                for h in range(HEADS):
                    for j in range(JT):
                        before, between, behind, end = slots[h][j]
                        for item in before:
                            make(item)
                        scores(h, j, 0)
                        for item in between:
                            make(item)
                        scores(h, j, 1)
                        for item in behind:
                            make(item)
                        if j > 0:
                            values(h, j - 1)
                        elif h > 0:
                            values(h - 1, JT - 1)
                        for item in end:
                            make(item)
                values(HEADS - 1, JT - 1)
                for item in unit_tail(last):
                    make(item)

            over_units(pe, unit)


_WEIGHTS = ("L0_conv_qkv_w", "L0_conv_proj_w", "L1_conv_proj_w", "L1_conv_out_w")


def lay_out(inputs):
    import numpy as np

    def f(name):
        return np.asarray(inputs[name])

    w1 = f("L1_conv_proj_w").reshape(HEADS, 3, D, C).transpose(1, 0, 2, 3).reshape(3 * C, C)
    b1 = f("L1_conv_proj_b").reshape(HEADS, 3, D).transpose(1, 0, 2).reshape(3 * C)
    layers = [
        (f("L0_conv_norm_w"), f("L0_conv_norm_b"), f("L0_conv_qkv_w"), f("L0_conv_qkv_b"), f("L0_conv_proj_w"), f("L0_conv_proj_b")),
        (f("L1_conv_gn_w"), f("L1_conv_gn_b"), w1, b1, f("L1_conv_out_w"), f("L1_conv_out_b")),
    ]
    weights = np.zeros((2, 8, P, 1024), np.float32)
    params = np.zeros((2, P, AHEAD + OWN), np.float32)
    for n, (gamma, beta, wqkv, bqkv, wo, bo) in enumerate(layers):
        wt = wqkv.T.reshape(KT, P, 3, C)
        for p in range(PAIRS):
            qk = wt[:, :, 0:2, p * P:(p + 1) * P]
            weights[n, p] = qk.transpose(1, 0, 2, 3).reshape(P, 1024)
        for i in range(2):
            weights[n, 4 + i] = wt[2 * i:2 * i + 2, :, 2, :].transpose(1, 0, 2).reshape(P, 1024)
            weights[n, 6 + i] = wo.T.reshape(KT, P, 2, 256)[:, :, i].transpose(1, 0, 2).reshape(P, 1024)
        bq, bk, bv = bqkv.reshape(3, PAIRS, P)
        params[n, :, GAMMA:GAMMA + KT] = gamma.reshape(KT, P).T
        params[n, :, BETA:BETA + KT] = beta.reshape(KT, P).T
        for p in range(PAIRS):
            at = 8 if p == 0 else AHEAD + 3 * (p - 1)
            params[n, :, at] = bq[p]
            params[n, :, at + 1] = bk[p]
            params[n, :D, at + 2] = bk[p, D:]
            params[n, D:, at + 2] = bk[p, :D]
        params[n, :, AHEAD + BV:AHEAD + BV + PAIRS] = bv.T
        params[n, :, AHEAD + BO:AHEAD + BO + KT] = bo.reshape(KT, P).T
    return weights, params


def kernel(**inputs):
    import numpy as np
    import concourse.bacc as bacc
    from concourse.bass_utils import run_bass_kernel_spmd as run

    x = np.asarray(inputs["x"])
    images = x.shape[0]
    weights, params = lay_out(inputs)
    arrays = {"x": x.reshape(images, C, T), "weights": weights, "params": params}
    nc = bacc.Bacc("TRN2", target_bir_lowering=False, num_devices=1)
    args = [nc.dram_tensor(n, a.shape, F32, kind="ExternalInput").ap() for n, a in arrays.items()]
    state = nc.dram_tensor("state", (3 * images, C, T), F32, kind="ExternalOutput").ap()
    build(nc, *args, state, 2 * images, images)
    r = run(nc, [arrays], core_ids=[0])
    return r.results[0]["state"][2 * images:].reshape(x.shape)
```

```python
from contextlib import ExitStack

import concourse.bass as bass
import concourse.mybir as mybir

F32 = mybir.dt.float32
F32R = mybir.dt.float32r
ALU = mybir.AluOpType
ACT = mybir.ActivationFunctionType
AX = mybir.AxisListType

C, T = 512, 1024
HEADS, D = 8, 64
P = 128
KT = C // P
JT = T // P
NH = 512
HALVES = T // NH
BANKS = 3
PAIRS = HEADS // 2
QUARTERS = 4
QP, QN = P // QUARTERS, T // QUARTERS
SPREAD_DMAS = QUARTERS * D // QP
GROUP = C // 32
EPS = 1e-5
SCALE = 1.0 / 8.0

GAMMA, BETA = 0, 4
AHEAD = 11
OWN = 17
BV, BO = 9, 13

STACK = [0, 2, 0, 1, 0, 2, 0, 1]

QK1, QK2, QK3, QK0, WV0, WV1, WO0, WO1 = range(8)
CHUNKS = 8
SLOT = [0, 1, 2, 0, 1, 2, 0, 1]
CHUNK_ROW = {QK0: 0, QK1: 1, QK2: 2, QK3: 3, WV0: 4, WV1: 5, WO0: 6, WO1: 7}
QK_CHUNK = [QK0, QK1, QK2, QK3]
PRO_CHUNKS = [QK0, WV0, WV1]
PRO = len(PRO_CHUNKS)

DRAINED_BY = {"q": "dve", "k": "dve", "max": "dve", "mrow": "act", "den": "act",
              "gm": "dve", "gv": "dve", "v": "act", "out": "dve"}
FOR_ACT, FOR_DVE = ("q", "k", "mrow", "den", "v"), ("max", "gm", "gv", "out")


def qk_items(pair):
    return [(kind, pair, n) for kind in "qk" for n in range(HALVES)]


def max_items(head):
    return [("max", head, i) for i in range(JT * HALVES)]


STATS_AT = {(3, 0): 0, (4, 0): 1, (5, 5): 2, (6, 0): 3}
GROUP_AT = {(3, 2): [("gm", 0)], (3, 3): [("gv", 0)], (4, 1): [("gm", 1)], (4, 3): [("gv", 1)],
            (5, 6): [("gm", 2)], (5, 7): [("gv", 2)], (6, 1): [("gm", 3)], (6, 2): [("gv", 3)]}
GAIN_AT = {(4, 0): 0, (4, 5): 1, (6, 2): 2, (6, 3): 3}
APPLY_AT = {(4, 1): 0, (4, 6): 1, (6, 3): 2, (6, 4): 3}
H_HIGH_AT = {(5, 1): 0, (5, 2): 1, (6, 4): 2, (6, 5): 3}
RSTD_AT = {(3, 3): [0], (4, 2): [1], (6, 0): [2], (6, 1): [3]}
H_LOW_AT = {(5, 0): 0, (5, 1): 1, (6, 3): 2, (6, 4): 3}

ADDED = {"dve": [1], "pool": [2, 3, 4, 5, 6, 7]}


def sum_of(tile):
    if tile == 0:
        return "dve", 0
    who = "dve" if tile in ADDED["dve"] else "pool"
    return who, ADDED[who].index(tile)


SPLIT_AT = {(0, 3): QK1, (1, 3): QK2, (1, 5): QK3, (3, 3): QK0, (3, 5): WV0, (7, 3): WV1}
SPLIT_AT_LAST = {(0, 3): QK1, (1, 3): QK2, (3, 3): QK3, (4, 3): WO0, (6, 3): WO1}


EVEN_STEPS = ["G,M,M,M", "G,M,M,M", "G,M,M,D", "G,M,M,M", "G,M,M,M", "G,R,,M", "G,M,,", "G,,R,"]
ODD_STEPS = [",,Q,Q", ",D,K,K", "G,,M,M", "G,M,M,M", "G,M,M,M", "GM,M,R,M", "GM,M,M,M", "GM,,,R"]
PIECES = 2
RECIP_AT = ({(3, 2): [0], (4, 1): [1]}, {(1, 0): [0, 1]})
NORMALIZE_AT = (6, 3)
ADD_AT = ({0: (2, 0)}, {0: (1, 1)})


def unit_slots(last):
    heads = []
    for h in range(HEADS):
        queues = {"D": [("den", h - 1, 0)] if h else [],
                  "Q": [("q", (h + 1) // 2, n) for n in range(HALVES)],
                  "K": [("k", (h + 1) // 2, n) for n in range(HALVES)],
                  "M": max_items(h + 1),
                  "R": [("mrow", h + 1, n) for n in range(HALVES)]}
        heads.append([])
        for j, step in enumerate(ODD_STEPS if h % 2 else EVEN_STEPS):
            slots = []
            for slot in step.split(","):
                items = []
                for kind in slot:
                    if kind == "G":
                        items += [] if last else [(g, kt, 0) for g, kt in GROUP_AT.get((h, j), [])]
                    elif kind == "D":
                        items += queues[kind]
                    elif not (last and h == HEADS - 1):
                        items.append(queues[kind].pop(0))
                slots.append(items)
            heads[-1].append(slots)
        if not (last and h == HEADS - 1):
            assert not queues["M"] and not queues["R"]
    return heads


def unit_steps(last):
    return [[[i for slot in step for i in slot] for step in head] for head in unit_slots(last)]


def unit_tail(last):
    tail = [("v", t, 0) for t in range(JT)] if not last else []
    tail.insert(min(len(tail), 2), ("den", HEADS - 1, 0))
    return tail + [("out", m, n) for m in range(KT) for n in range(HALVES)]


def unit_items(last):
    return [i for row in unit_steps(last) for step in row for i in step] + unit_tail(last)


def prologue_items():
    items = []
    for kt in range(KT):
        items += [("gm", kt, 0), ("gv", kt, 0)]
    items += qk_items(0)
    for t in range(JT):
        items += [("v", t, 0)] + max_items(0)[t * HALVES:(t + 1) * HALVES]
    return items + [("mrow", 0, n) for n in range(HALVES)]


def drained(items, who):
    return sum(DRAINED_BY[k] == who for k, _, _ in items)


def of_kinds(items, kinds):
    return sum(k in kinds for k, _, _ in items)


class Count:

    def __init__(self, first, each):
        self.first, self.each = first, each

    def after(self, u, n):
        return u * self.each + (self.first + n)


def build(nc, x, weights, params, state, units, images):
    loop_items, pro_items = unit_items(False), prologue_items()

    DRAINED = {who: Count(drained(pro_items, who), drained(loop_items, who)) for who in ("dve", "act")}
    FILLED = {who: Count(of_kinds(pro_items, kinds), of_kinds(loop_items, kinds))
              for who, kinds in (("act", FOR_ACT), ("dve", FOR_DVE))}
    QKS = Count(4, 16)
    HIS = Count(8, 32)
    STEPS = Count(0, HEADS * JT)
    HALF_STEPS = Count(0, HEADS * JT * HALVES)
    ADDS = {who: Count(0, len(tiles) * HEADS) for who, tiles in ADDED.items()}
    NORMED = Count(0, HEADS)
    RECIPS = Count(0, PIECES * HEADS)
    SPREADS = Count(0, 16 * SPREAD_DMAS * HEADS)
    PAIRS_SPLIT = Count(0, PAIRS)
    MAXIMA = Count(2, 2 * HEADS)
    CHUNKS_SPLIT = Count(PRO, CHUNKS)
    GN = Count(KT, KT)
    RESIDS = [Count(0, 16 * len(range(b, KT, 3))) for b in range(3)]
    STORES = [Count(16 * len(range(b, images, 3)), RESIDS[b].each) for b in range(3)]
    assert images >= 3

    ctx = ExitStack()

    def sb(name, shape, dt=F32):
        return ctx.enter_context(nc.sbuf_tensor(name, shape, dt))

    def pb(name, shape):
        return ctx.enter_context(nc.psum_tensor(name, shape, F32))

    def sem(name):
        return ctx.enter_context(nc.semaphore(name))

    with ctx:
        x_tile = [sb(f"x_tile{i}", [P, T]) for i in range(2)]
        h_hi = sb("h_hi", [P, KT, T], F32R)
        h_lo = sb("h_lo", [P, KT, T], F32R)
        v_sb = sb("v_sb", [P, JT, C])
        w_stage = [sb(f"w_stage{i}", [P, 1024]) for i in range(2)]
        w_hi = sb("w_hi", [P, 3, 1024], F32R)
        w_lo = sb("w_lo", [P, 3, 1024], F32R)
        q_hh = [sb(f"q_hh{i}", [P, T], F32R) for i in range(3)]
        q_lm = [sb(f"q_lm{i}", [D + 1, T], F32R) for i in range(3)]
        k_hl = [sb(f"k_hl{i}", [P, T], F32R) for i in range(3)]
        k_h1 = [sb(f"k_h1{i}", [D + 1, T], F32R) for i in range(3)]
        probs = [sb(f"probs{i}", [P, T]) for i in range(4)]
        sum_dve = sb("sum_dve", [P, T])
        sum_pool = sb("sum_pool", [P, T])
        dens = sb("dens", [P, QN])
        recips = sb("recips", [P, NH])
        o_nat = sb("o_nat", [P, T])
        o_hi = sb("o_hi", [P, PAIRS, T], F32R)
        o_lo = sb("o_lo", [P, PAIRS, T], F32R)
        resid = [*x_tile, sb("resid", [P, T])]
        first_x = [*resid, o_nat]
        ahead = sb("ahead", [P, AHEAD])
        own = sb("own", [P, OWN])
        ident = sb("ident", [P, P])
        ident_r = sb("ident_r", [P, P], F32R)
        group_avg = sb("group_avg", [P, P])
        ones = sb("ones", [P, QP])
        mx = sb("mx", [P, JT, HALVES])
        mcol = sb("mcol", [P, JT], F32R)
        stats = sb("stats", [P, HALVES, 6])
        meanvar = sb("meanvar", [P, 2])
        gmean = [sb(f"gmean{i}", [P, 1]) for i in range(2)]
        spread_sq = sb("spread_sq", [P, 1])
        veps = [sb(f"veps{i}", [P, 1]) for i in range(2)]
        rstd = [sb(f"rstd{i}", [P, 1]) for i in range(2)]
        gain = [sb(f"gain{i}", [P, 1]) for i in range(2)]
        shift = [sb(f"shift{i}", [P, 1]) for i in range(2)]
        minus_half = sb("minus_half", [P, 1])
        pace = sb("pace", [P, 1])

        s_ps = [pb(f"s_ps{i}", [P, NH]) for i in range(BANKS)]
        work = [pb(f"work{i}", [P, NH]) for i in range(BANKS)]
        o_ps = [pb(f"o_ps{i}", [P, NH]) for i in range(2)]

        x_loaded = [sem(f"x_loaded{i}") for i in range(2)]
        first_x_loaded = [sem(f"first_x_loaded{i}") for i in range(2)]
        w_loaded = [sem(f"w_loaded{i}") for i in range(2)]
        resid_loaded = [sem(f"resid_loaded{i}") for i in range(3)]
        ahead_loaded = sem("ahead_loaded")
        recips_spread = sem("recips_spread")
        own_loaded = sem("own_loaded")
        stored = [sem(f"stored{i}") for i in range(3)]
        filled = {"act": sem("filled_for_act"), "dve": sem("filled_for_dve")}
        scores_made = sem("scores_made")
        values_used = sem("values_used")
        act_drained = sem("act_drained")
        hi_made = sem("hi_made")
        hi_copied = sem("hi_copied")
        w_hi_made = sem("w_hi_made")
        applied = sem("applied")
        normalized = sem("normalized")
        exps_done = sem("exps_done")
        o_hi_made = sem("o_hi_made")
        dve_drained = sem("dve_drained")
        shifts_made = sem("shifts_made")
        consts_dve = sem("consts_dve")
        adds_dve = sem("adds_dve")
        maxima_made = sem("maxima_made")
        recips_made = sem("recips_made")
        o_normed = sem("o_normed")
        stats_parts = sem("stats_parts")
        spread_steps = sem("spread_steps")
        gains_made = sem("gains_made")
        stats_made = sem("stats_made")
        spread_made = sem("spread_made")
        consts_pool = sem("consts_pool")
        masks = sem("masks")
        adds_pool = sem("adds_pool")
        w_split = sem("w_split")
        h_made = sem("h_made")
        o_lo_made = sem("o_lo_made")
        rstd_made = sem("rstd_made")

        block = ctx.enter_context(nc.Block())

        def w_tiles(chunk):
            n = 2 if chunk in (WV0, WV1) else 4
            return (w_hi[:, SLOT[chunk], :].rearrange("p (k c) -> p k c", k=n),
                    w_lo[:, SLOT[chunk], :].rearrange("p (k c) -> p k c", k=n))

        def qk_params(kind, pair):
            if pair == 0:
                return ahead, 8 + (kind == "k")
            return own, 3 * (pair - 1) + (kind == "k")

        def chunk_place(i, last):
            return QK3 + 1 + i - WO0 if last and i >= WO0 else i

        def over_units(eng, body):
            if units > 1:
                with eng.Fori(0, units - 1) as u:
                    body(u, False)
            body(units - 1, True)

        @block.sync
        def _(sp):
            def load_chunk(n, nth, row, first):
                if not first:
                    sp.wait_ge(w_split, nth)
                sp.dma_start(w_stage[n][:, :], row).then_inc(w_loaded[n], 16)

            sp.dma_start(ahead[:, :], params[0, :, 0:AHEAD]).then_inc(ahead_loaded, 16)
            for kt in range(KT):
                sp.dma_start(first_x[kt][:, :], x[0, kt * P:(kt + 1) * P, :]).then_inc(
                    (x_loaded + first_x_loaded)[kt], 16)
                if kt % 2:
                    load_chunk((kt // 2 + 1) % 2, kt // 2, weights[0, CHUNK_ROW[PRO_CHUNKS[kt // 2]]], True)
            load_chunk(1, 1, weights[0, CHUNK_ROW[PRO_CHUNKS[2]]], False)
            for b in range(images):
                sp.dma_start(state[b], x[b]).then_inc(stored[b % 3], 16)

            def unit(u, last):
                def held(value):
                    return value if isinstance(value, int) else sp.snap(value)

                layer, here, made = held(u // images), held(u + 0), held(u + images)
                if not last:
                    after, nxt = held((u + 1) // images), held(u + 1)
                items = unit_items(last)
                splits = [held(CHUNKS_SPLIT.after(u, i - 1)) for i in range(CHUNKS if not last else QK3 + 3)]
                gn_done = {k: held(GN.after(u, k)) for k in (0, 1, 2, KT)} if not last else {}
                outs = [held(DRAINED["dve"].after(u, drained(items[:items.index(("out", m, HALVES - 1)) + 1], "dve")))
                        for m in range(KT)]
                recip = [held(RECIPS.after(u, PIECES * (h + 1))) for h in range(HEADS)]
                stores = [held(STORES[m % 3].after(u, 16 * (m // 3 + 1))) for m in range(KT if last else KT - 3)]
                earlier = [held(STORES[b].after(u, 0)) for b in range(3)]

                def chunk(i):
                    of = after if i in (QK0, WV0, WV1) else layer
                    load_chunk(i % 2, splits[i], weights[of, CHUNK_ROW[i]], False)

                def x_load(kt):
                    sp.dma_start(x_tile[kt % 2][:, :], state[nxt, kt * P:(kt + 1) * P, :]).then_inc(x_loaded[kt % 2], 16)

                def rows(m):
                    return slice(m * P, (m + 1) * P)

                def spread(*heads):
                    for h in heads:
                        sp.wait_ge(recips_made, recip[h])
                        for c in range(QUARTERS):
                            half, part = divmod(c, QUARTERS // HALVES)
                            for row in range(half * D, (half + 1) * D, QP):
                                sp.dma_start(recips[row:row + QP, part * QN:(part + 1) * QN],
                                             dens[c * QP:(c + 1) * QP, :]).then_inc(recips_spread, 16)

                chunk(QK1)
                sp.wait_ge(stored[0], earlier[0])
                sp.dma_start(own[:, :], params[layer, :, AHEAD:]).then_inc(own_loaded, 16)
                chunk(QK2)
                chunk(QK3)
                spread(0)
                if not last:
                    chunk(QK0)
                    sp.wait_ge(stored[1], earlier[1])
                    sp.dma_start(ahead[:, :], params[after, :, 0:AHEAD]).then_inc(ahead_loaded, 16)
                    sp.wait_ge(stored[2], earlier[2])
                    sp.wait_ge(h_made, gn_done[0])
                    x_load(0)
                    x_load(1)
                    chunk(WV0)
                    spread(1, 2)
                    chunk(WV1)
                    chunk(WO0)
                    spread(3, 4)
                    sp.wait_ge(h_made, gn_done[1])
                    x_load(2)
                    sp.wait_ge(h_made, gn_done[2])
                    x_load(3)
                    spread(5, 6)
                    chunk(WO1)
                    spread(7)
                    sp.wait_ge(h_made, gn_done[KT])
                else:
                    for i, heads in ((WO0, (1, 2)), (WO1, (3, 4, 5, 6, 7))):
                        place = chunk_place(i, last)
                        load_chunk(place % 2, splits[place], weights[layer, CHUNK_ROW[i]], False)
                        spread(*heads)
                    for b in range(1, 3):
                        sp.wait_ge(stored[b], earlier[b])

                def load(m):
                    if m >= 3:
                        sp.wait_ge(stored[m % 3], stores[m - 3])
                    sp.dma_start(resid[m % 3][:, :], state[here, rows(m), :]).then_inc(resid_loaded[m % 3], 16)

                for m in range(3):
                    load(m)
                for m in range(KT):
                    if m == 1:
                        load(3)
                    sp.wait_ge(dve_drained, outs[m])
                    sp.dma_start(state[made, rows(m), :], resid[m % 3][:, :]).then_inc(stored[m % 3], 16)
                if last:
                    for m in range(1, KT):
                        sp.wait_ge(stored[m % 3], stores[m])

            over_units(sp, unit)

        @block.gpsimd
        def _(pool):
            nc.gpsimd.memset(ident[:, :], 0.0).then_inc(masks, 1)
            nc.gpsimd.memset(group_avg[:, :], 1.0 / GROUP).then_inc(masks, 1)
            nc.gpsimd.memset(ones[:, :], 1.0).then_inc(consts_pool, 1)
            nc.gpsimd.memset(minus_half[:, :], -0.5).then_inc(consts_pool, 1)
            pool.wait_ge(masks, 2)
            nc.gpsimd.affine_select(out=ident[:, :], in_=ident[:, :], compare_op=ALU.not_equal, fill=1.0,
                                    base=0, pattern=[[-1, P]], channel_multiplier=1).then_inc(consts_pool, 1)
            by_group = group_avg[:, :].rearrange("p (g c) -> p g c", c=GROUP)
            nc.gpsimd.affine_select(out=by_group, in_=by_group, compare_op=ALU.is_ge, fill=0.0, base=0,
                                    pattern=[[-GROUP, P // GROUP], [0, GROUP]], channel_multiplier=1).then_inc(masks, 1)
            pool.wait_ge(masks, 3)
            nc.gpsimd.affine_select(out=by_group, in_=by_group, compare_op=ALU.is_ge, fill=0.0, base=GROUP - 1,
                                    pattern=[[GROUP, P // GROUP], [0, GROUP]], channel_multiplier=-1).then_inc(consts_pool, 1)
            pool.wait_ge(consts_pool, 4)

            def w_low(chunk, stage, nth):
                pool.wait_ge(w_hi_made, nth + 1)
                nc.gpsimd.tensor_tensor(w_lo[:, SLOT[chunk], :], w_stage[stage][:, :],
                                        w_hi[:, SLOT[chunk], :].bitcast(F32), ALU.subtract).then_inc(w_split, 1)

            def h_low(kt, nth, tile):
                pool.wait_ge(applied, nth + 1)
                nc.gpsimd.tensor_tensor(h_lo[:, kt, :], tile[:, :], h_hi[:, kt, :].bitcast(F32),
                                        ALU.subtract).then_inc(h_made, 1)

            def rstd_of(kt, drained_to):
                pool.wait_ge(dve_drained, drained_to)
                nc.gpsimd.tensor_tensor(rstd[kt % 2][:, :], veps[kt % 2][:, :], minus_half[:, :], ALU.pow).then_inc(rstd_made, 1)

            for kt in range(KT + 1):
                if kt < KT:
                    rstd_of(kt, drained(pro_items[:pro_items.index(("gv", kt, 0)) + 1], "dve"))
                if kt == 0:
                    w_low(QK0, 1, 0)
                else:
                    h_low(kt - 1, kt - 1, first_x[kt - 1])
                if kt == KT - 1:
                    w_low(WV0, 0, 1)
            w_low(WV1, 1, 2)

            def unit(u, last):
                items = unit_items(last)

                splits = SPLIT_AT_LAST if last else SPLIT_AT

                def w_low_here(i):
                    place = chunk_place(i, last)
                    w_low(i, place % 2, CHUNKS_SPLIT.after(u, place))

                def o_low(pair):
                    pool.wait_ge(o_hi_made, PAIRS_SPLIT.after(u, pair + 1))
                    nc.gpsimd.tensor_tensor(o_lo[:, pair, :], o_nat[:, :], o_hi[:, pair, :].bitcast(F32),
                                            ALU.subtract).then_inc(o_lo_made, 1)

                def add(h, k):
                    j = ADDED["pool"][k]
                    if k == 0:
                        pool.wait_ge(adds_dve, ADDS["dve"].after(u, len(ADDED["dve"]) * (h + 1)))
                    if k == 0 and h > 0:
                        upto = items[:items.index(("den", h - 1, 0)) + 1]
                        pool.wait_ge(filled["act"], FILLED["act"].after(u, of_kinds(upto, FOR_ACT)))
                    if k > 0:
                        pool.wait_ge(adds_pool, ADDS["pool"].after(u, len(ADDED["pool"]) * h + k))
                    pool.wait_ge(exps_done, HALF_STEPS.after(u, (h * JT + j + 1) * HALVES))
                    first = sum_dve if k == 0 else sum_pool
                    nc.gpsimd.tensor_tensor(sum_pool[:, :], first[:, :], probs[j % 4][:, :], ALU.add).then_inc(adds_pool, 1)

                for h in range(HEADS):
                    if h in (3, 5, 7):
                        o_low(h // 2 - 1)
                    for k in range(len(ADDED["pool"])):
                        if not last:
                            for kt in RSTD_AT.get((h, k), []):
                                upto = items[:items.index(("gv", kt, 0)) + 1]
                                rstd_of(kt, DRAINED["dve"].after(u, drained(upto, "dve")))
                            if (h, k) in H_LOW_AT:
                                kt = H_LOW_AT[h, k]
                                h_low(kt, GN.after(u, kt), x_tile[kt % 2])
                        if (h, ADDED["pool"][k]) in splits:
                            w_low_here(splits[h, ADDED["pool"][k]])
                        add(h, k)
                if not last:
                    w_low_here(WO0)
                o_low(PAIRS - 1)
                if not last:
                    w_low_here(WO1)

            over_units(pool, unit)

        @block.scalar
        def _(act):
            def filled_of(kinds_items, item):
                upto = kinds_items[:kinds_items.index(item) + 1]
                return of_kinds(upto, FOR_ACT)

            def qk_hi(item, bank, heads, col, par, his, nth):
                kind, _, n = item
                for half, s in enumerate(heads):
                    rows = slice(half * D, (half + 1) * D)
                    src, bias = work[bank][rows, :], par[rows, col:col + 1]
                    cols = slice(n * NH, (n + 1) * NH)
                    out = q_hh[s][rows, cols] if kind == "q" else k_hl[s][0:D, cols]
                    nc.scalar.activation(out, src, ACT.Identity, bias=bias).then_inc(hi_made, 1)
                for half, s in enumerate(heads):
                    act.wait_ge(hi_made, his(nth - 1 + half))
                    if kind == "q":
                        rows, other = [slice(k * D, (k + 1) * D) for k in (half, 1 - half)]
                        done = nc.scalar.copy(q_hh[s][other, cols], q_hh[s][rows, cols])
                    else:
                        done = nc.scalar.copy(k_h1[s][0:D, cols], k_hl[s][0:D, cols])
                done.then_inc(hi_copied, 1)

            def mrow(item, bank, s):
                n = item[2]
                nc.scalar.activation(q_lm[s][D:D + 1, n * NH:(n + 1) * NH], work[bank][0:1, :], ACT.Copy,
                                     scale=-1.0).then_inc(act_drained, 1)

            def take(items, item, at, his, normed=None):
                kind, a, n = item
                bank = items.index(item) % BANKS
                act.wait_ge(filled["act"], at(filled_of(items, item)))
                if kind in "qk":
                    pair = a % PAIRS
                    par, col = qk_params(kind, pair)
                    nth = 2 * of_kinds(items[:items.index(item)], "qk") + 2
                    qk_hi(item, bank, (STACK[2 * pair], STACK[2 * pair + 1]), col, par, his, nth)
                elif kind == "mrow":
                    mrow(item, bank, STACK[a % HEADS])
                elif kind == "den":
                    if a > 0:
                        act.wait_ge(o_normed, normed(a))
                    nc.scalar.copy(dens[:, :], work[bank][:, 0:QN]).then_inc(act_drained, 1)
                else:
                    nc.scalar.copy(v_sb[:, a, :], work[bank][:, :]).then_inc(act_drained, 1)

            def half_of(n):
                return slice(n * NH, (n + 1) * NH)

            def w_high(chunk, stage, loads, n):
                if n == 0:
                    act.wait_ge(w_loaded[stage], loads)
                done = nc.scalar.copy(w_hi[:, SLOT[chunk], half_of(n)], w_stage[stage][:, half_of(n)])
                if n == HALVES - 1:
                    done.then_inc(w_hi_made, 1)

            def gn_apply(kt, nth, n, tiles):
                if n == 0:
                    act.wait_ge(shifts_made, nth + 1)
                tile = tiles[kt][:, half_of(n)]
                nc.scalar.activation(tile, tile, ACT.Identity, bias=shift[kt % 2][:, :],
                                     scale=gain[kt % 2][:, :]).then_inc(normalized, 1)

            def gn_high(kt, nth, n, tiles):
                act.wait_ge(normalized, HALVES * nth + (n + 1))
                done = nc.scalar.copy(h_hi[:, kt, half_of(n)], tiles[kt][:, half_of(n)])
                if n == HALVES - 1:
                    done.then_inc(applied, 1)

            act.wait_ge(ahead_loaded, 16)
            for n in range(HALVES):
                w_high(QK0, 1, 16, n)
            for kt in range(KT):
                for n in range(HALVES):
                    gn_apply(kt, kt, n, first_x)
                for n in range(HALVES):
                    gn_high(kt, kt, n, first_x)
                if kt == 1:
                    for n in range(HALVES):
                        w_high(WV0, 0, 16, n)
            act.wait_ge(w_split, 1)
            for n in range(HALVES):
                w_high(WV1, 1, 32, n)
            for item in pro_items:
                if item[0] in FOR_ACT:
                    take(pro_items, item, lambda n: n, lambda n: n)

            def unit(u, last):
                items, slots = unit_items(last), unit_slots(last)
                splits = SPLIT_AT_LAST if last else SPLIT_AT

                def at(n):
                    return FILLED["act"].after(u, n)

                def normed(n):
                    return NORMED.after(u, n)

                def his(n):
                    return HIS.after(u, n)

                def o_high(pair, n):
                    if n == 0:
                        act.wait_ge(o_normed, NORMED.after(u, 2 * pair + 2))
                    nc.scalar.activation(o_hi[:, pair, half_of(n)], o_nat[:, half_of(n)], ACT.Identity,
                                         bias=own[:, BV + pair:BV + pair + 1])

                def o_biased(pair, n):
                    done = nc.scalar.activation(o_nat[:, half_of(n)], o_nat[:, half_of(n)], ACT.Identity,
                                                bias=own[:, BV + pair:BV + pair + 1])
                    if n == HALVES - 1:
                        done.then_inc(o_hi_made, 1)

                def last_pair():
                    for n in range(HALVES):
                        o_high(PAIRS - 1, n)
                    for n in range(HALVES):
                        o_biased(PAIRS - 1, n)

                def beside(h, j, n):
                    if j == JT - 1 and h in (2, 4, 6):
                        o_high(h // 2 - 1, n)
                    if j == 0 and h in (3, 5, 7):
                        o_biased(h // 2 - 1, n)
                    if (h, j + 1) in splits:
                        w_high_here(splits[h, j + 1], n)
                    if not last and (h, j) in APPLY_AT:
                        kt = APPLY_AT[h, j]
                        gn_apply(kt, GN.after(u, kt), n, x_tile * 2)
                    if not last and (h, j) in H_HIGH_AT:
                        kt = H_HIGH_AT[h, j]
                        gn_high(kt, GN.after(u, kt), n, x_tile * 2)

                def w_high_here(i, n):
                    if n > 0:
                        w_high(i, chunk_place(i, last) % 2, None, n)
                        return
                    place = chunk_place(i, last)
                    if i in (QK1, QK2, QK3):
                        act.wait_ge(filled["act"], FILLED["act"].after(u, 0))
                        act.wait_ge(filled["dve"], FILLED["dve"].after(u, 0))
                    else:
                        user = {QK0: ("k", 1, 1), WV0: ("k", 2, 1), WV1: ("k", 3, 1),
                                WO0: ("k", 1 if last else 4, 1), WO1: ("k", 2, 1) if last else ("v", JT - 1, 0)}[i]
                        upto = items[:items.index(user) + 1]
                        act.wait_ge(filled["act"], FILLED["act"].after(u, of_kinds(upto, FOR_ACT)))
                    w_high(i, place % 2, Count(16 * (1 + place % 2), 64).after(u, 16 * (place // 2 + 1)), n)

                def exp(h, j, n):
                    if n == 0 and (h > 0 or j >= 4):
                        act.wait_ge(values_used, STEPS.after(u, h * JT + j - 3))
                        who, k = sum_of((j - 4) % JT)
                        head = h if j >= 4 else h - 1
                        act.wait_ge(adds_dve if who == "dve" else adds_pool,
                                    ADDS[who].after(u, len(ADDED[who]) * head + k + 1))
                    g = (h * JT + j) * HALVES + n
                    act.wait_ge(scores_made, HALF_STEPS.after(u, g + 1))
                    nc.scalar.activation(probs[j % 4][:, half_of(n)], s_ps[g % BANKS][:, :], ACT.Exp,
                                         scale=SCALE).then_inc(exps_done, 1)

                for h in range(HEADS):
                    if h == 1:
                        act.wait_ge(own_loaded, Count(0, 16).after(u, 16))
                    if h == HEADS - 1 and not last:
                        act.wait_ge(ahead_loaded, Count(16, 16).after(u, 16))
                    for j in range(JT):
                        before, between, behind, end = slots[h][j]
                        for item in before + between + behind:
                            if item[0] in FOR_ACT and (item not in behind or item[0] == "mrow"):
                                take(items, item, at, his, normed)
                        exp(h, j, 0)
                        if (h, j) != (0, 0):
                            beside(*divmod(h * JT + j - 1, JT), 1)
                        exp(h, j, 1)
                        for item in behind + end:
                            if item[0] in FOR_ACT and (item not in behind or item[0] != "mrow"):
                                take(items, item, at, his, normed)
                        beside(h, j, 0)
                beside(HEADS - 1, JT - 1, 1)
                if not last:
                    for n in range(HALVES):
                        w_high_here(WO0, n)
                for item in unit_tail(last):
                    if item[0] in FOR_ACT:
                        take(items, item, at, his, normed)
                    if item == ("v", 4, 0):
                        last_pair()
                if last:
                    last_pair()
                else:
                    for n in range(HALVES):
                        w_high_here(WO1, n)

            over_units(act, unit)

        @block.vector
        def _(dve):
            v = nc.vector

            def filled_of(items, item):
                upto = items[:items.index(item) + 1]
                return of_kinds(upto, FOR_DVE)

            def qks_of(items, item):
                upto = items[:items.index(item) + 1]
                return of_kinds(upto, ("q", "k"))

            def qk_lo(item, bank, heads, col, par, his):
                kind, _, n = item
                cols = slice(n * NH, (n + 1) * NH)
                for half, s in enumerate(heads):
                    rows = slice(half * D, (half + 1) * D)
                    src = work[bank][rows, :]
                    if kind == "q":
                        hi, bias, out = q_hh[s][rows, cols], par[rows, col:col + 1], q_lm[s][0:D, cols]
                    else:
                        hi, bias, out = k_hl[s][0:D, cols], par[0:D, col + half:col + half + 1], k_hl[s][D:P, cols]
                    dve.wait_ge(hi_made, his[half])
                    done = v.scalar_tensor_tensor(out=out, in0=src, scalar=bias, in1=hi.bitcast(F32),
                                                  op0=ALU.add, op1=ALU.subtract)
                done.then_inc(dve_drained, 1)

            def gn_stats(tile, loaded, nth_load, nth):
                dve.wait_ge(loaded, nth_load)
                for n in range(HALVES):
                    v.bn_stats(stats[:, n, :], tile[:, n * NH:(n + 1) * NH]).then_inc(stats_parts, 1)
                dve.wait_ge(stats_parts, 2 * nth + 2)
                v.memset(pace[:, :], 0.0)
                v.bn_aggr(meanvar[:, :], stats[:, :, :]).then_inc(stats_made, 1)

            def gn_mean(kt, bank, nth):
                v.tensor_tensor(spread_sq[:, :], meanvar[:, 0:1], work[bank][:, 0:1], ALU.subtract).then_inc(spread_steps, 1)
                v.tensor_copy(gmean[kt % 2][:, :], work[bank][:, 0:1]).then_inc(dve_drained, 1)
                dve.wait_ge(spread_steps, 2 * nth + 1)
                v.tensor_tensor(spread_sq[:, :], spread_sq[:, :], spread_sq[:, :], ALU.mult).then_inc(spread_steps, 1)
                dve.wait_ge(spread_steps, 2 * nth + 2)
                v.tensor_tensor(spread_sq[:, :], spread_sq[:, :], meanvar[:, 1:2], ALU.add).then_inc(spread_made, 1)

            def gn_var(kt, bank):
                done = v.tensor_scalar(veps[kt % 2][:, :], work[bank][:, 0:1], EPS, None, ALU.add)
                done.then_inc(dve_drained, 1)

            def gn_gain(kt, nth):
                dve.wait_ge(rstd_made, nth + 1)
                v.tensor_tensor(gain[kt % 2][:, :], rstd[kt % 2][:, :], ahead[:, GAMMA + kt:GAMMA + kt + 1],
                                ALU.mult).then_inc(gains_made, 1)
                dve.wait_ge(gains_made, nth + 1)
                v.scalar_tensor_tensor(out=shift[kt % 2][:, :], in0=gmean[kt % 2][:, :], scalar=gain[kt % 2][:, :],
                                       in1=ahead[:, BETA + kt:BETA + kt + 1], op0=ALU.mult, op1=ALU.subtract,
                                       reverse1=True).then_inc(shifts_made, 1)

            def maximum(item, bank):
                t, n = divmod(item[2], HALVES)
                ins = v.reduce_max(mx[:, t, n:n + 1], work[bank][:, :], axis=AX.X)
                ins.then_inc(dve_drained, 1)

            def maxima(half, drained_to):
                dve.wait_ge(dve_drained, drained_to)
                rows = slice(half * JT // 2, (half + 1) * JT // 2)
                v.tensor_tensor(mcol[:, rows], mx[:, rows, 0], mx[:, rows, 1], ALU.max).then_inc(maxima_made, 1)

            def take(items, item, at, u):
                kind, a, n = item
                bank = items.index(item) % BANKS
                upto = drained(items[:items.index(item) + 1], "dve")
                if kind in "qk":
                    pair = a % PAIRS
                    par, col = qk_params(kind, pair)
                    his = [at("hi", 2 * qks_of(items, item) - 1 + half) for half in range(2)]
                    qk_lo(item, bank, (STACK[2 * pair], STACK[2 * pair + 1]), col, par, his)
                    return
                dve.wait_ge(filled["dve"], at("filled", filled_of(items, item)))
                if kind == "max":
                    maximum(item, bank)
                    if (n + 1) % JT == 0:
                        maxima(n // JT, at("drained", upto))
                elif kind == "gm":
                    gn_mean(a, bank, at("gn", a))
                elif kind == "gv":
                    gn_var(a, bank)
                elif kind == "out":
                    tile, cols = resid[a % 3], slice(n * NH, (n + 1) * NH)
                    if n == 0:
                        dve.wait_ge(resid_loaded[a % 3], RESIDS[a % 3].after(u, 16 * (a // 3 + 1)))
                    done = v.scalar_tensor_tensor(out=tile[:, cols], in0=work[bank][:, :],
                                                  scalar=own[:, BO + a:BO + a + 1], in1=tile[:, cols],
                                                  op0=ALU.add, op1=ALU.add)
                    done.then_inc(dve_drained, 1)

            def before_loop(what, n):
                return n

            for s in range(3):
                v.memset(k_h1[s][D:D + 1, :].bitcast(F32), 1.0).then_inc(consts_dve, 1)
            dve.wait_ge(consts_pool, 4)
            v.tensor_copy(ident_r[:, :], ident[:, :]).then_inc(consts_dve, 1)
            dve.wait_ge(ahead_loaded, 16)
            for kt in range(KT + 1):
                if kt < KT:
                    gn_stats(first_x[kt], (x_loaded + first_x_loaded)[kt], 16, kt)
                if kt > 0:
                    if kt > 2:
                        dve.wait_ge(applied, kt - 2)
                    gn_gain(kt - 1, kt - 1)
                if kt < KT:
                    take(pro_items, ("gm", kt, 0), before_loop, 0)
                    take(pro_items, ("gv", kt, 0), before_loop, 0)
            for item in pro_items:
                if item[0] in ("q", "k", "max"):
                    take(pro_items, item, before_loop, 0)

            def unit(u, last):
                items, steps = unit_items(last), unit_steps(last)

                def at(what, n):
                    return {"hi": HIS, "filled": FILLED["dve"], "drained": DRAINED["dve"], "gn": GN}[what].after(u, n)

                def add(h, k):
                    j = ADDED["dve"][k]
                    if h > 0:
                        dve.wait_ge(adds_pool, ADDS["pool"].after(u, len(ADDED["pool"]) * (h - 1) + 1))
                    dve.wait_ge(exps_done, HALF_STEPS.after(u, (h * JT + j + 1) * HALVES))
                    v.tensor_tensor(sum_dve[:, :], probs[0][:, :], probs[j % 4][:, :], ALU.add).then_inc(adds_dve, 1)

                def reciprocal(h, piece):
                    if piece == 0:
                        upto = items[:items.index(("den", h, 0)) + 1]
                        dve.wait_ge(act_drained, DRAINED["act"].after(u, drained(upto, "act")))
                    cols = slice(piece * P, (piece + 1) * P)
                    v.reciprocal(dens[:, cols], dens[:, cols]).then_inc(recips_made, 1)

                def normalize(h):
                    dve.wait_ge(recips_spread, SPREADS.after(u, 16 * SPREAD_DMAS * (h + 1)))
                    if h >= 2 and h % 2 == 0:
                        dve.wait_ge(o_lo_made, PAIRS_SPLIT.after(u, h // 2))
                    for half in range(HALVES):
                        rows = slice(half * D, (half + 1) * D)
                        done = v.tensor_tensor(o_nat[h % 2 * D:(h % 2 + 1) * D, half * NH:(half + 1) * NH],
                                               o_ps[h % 2][rows, :], recips[rows, :], ALU.mult)
                    done.then_inc(o_normed, 1)

                for h in range(HEADS):
                    if h == 1:
                        dve.wait_ge(own_loaded, Count(0, 16).after(u, 16))
                    if h == 3 and not last:
                        dve.wait_ge(ahead_loaded, Count(16, 16).after(u, 16))
                    for j in range(JT):
                        if not last and (h, j) in STATS_AT:
                            kt = STATS_AT[h, j]
                            gn_stats(x_tile[kt % 2], x_loaded[kt % 2], Count(16, 32).after(u, 16 * (kt // 2 + 1)), GN.after(u, kt))
                        mine = [i for i in steps[h][j] if DRAINED_BY[i[0]] == "dve"]
                        adds = [k for k, (step, _) in ADD_AT[h % 2].items() if step == j]
                        for n, item in enumerate(mine):
                            for k in adds:
                                if ADD_AT[h % 2][k][1] == n:
                                    add(h, k)
                            for piece in RECIP_AT[h % 2].get((j, n), []) if h > 0 else []:
                                reciprocal(h - 1, piece)
                            take(items, item, at, u)
                        if not mine:
                            for k in adds:
                                add(h, k)
                        if not last and (h, j) in GAIN_AT:
                            kt = GAIN_AT[h, j]
                            gn_gain(kt, GN.after(u, kt))
                        if last and h == HEADS - 1 and j == 1:
                            for piece in range(PIECES):
                                reciprocal(h - 1, piece)
                        if h > 0 and j == NORMALIZE_AT[h % 2]:
                            normalize(h - 1)
                for piece in range(PIECES):
                    reciprocal(HEADS - 1, piece)
                normalize(HEADS - 1)
                for item in unit_tail(last):
                    if item[0] == "out":
                        take(items, item, at, u)

            over_units(dve, unit)

        @block.tensor
        def _(pe):
            mm = nc.tensor.matmul

            def three(out, w, x, k, n, flip=False):
                (wh, wl), (xh, xl) = w, x
                pairs = [(xh, wh), (xh, wl), (xl, wh)] if flip else [(wh, xh), (wl, xh), (wh, xl)]
                for i, (a, b) in enumerate(pairs):
                    last = mm(out, a, b, start=(k == 0 and i == 0), stop=(k == n - 1 and i == 2))
                return last

            def fill(items, item, prior, u):
                kind, a, n = item
                pos = items.index(item)
                bank = work[pos % BANKS]
                if pos < BANKS:
                    for before in (loop_items, pro_items) if prior is not None else ():
                        at = max(i for i in range(len(before)) if i % BANKS == pos)
                        who = DRAINED_BY[before[at][0]]
                        pe.wait_ge(dve_drained if who == "dve" else act_drained, prior(who, -drained(before[at + 1:], who)))
                else:
                    who = DRAINED_BY[items[pos - BANKS][0]]
                    upto = drained(items[:pos - BANKS + 1], who)
                    pe.wait_ge(dve_drained if who == "dve" else act_drained, upto if prior is None else prior(who, upto))
                if kind in "qk":
                    wh, wl = w_tiles(QK_CHUNK[a % PAIRS])
                    cols = slice(0, P) if kind == "q" else slice(P, 2 * P)
                    for k in range(KT):
                        if kind == "q" and n == 0 and a in (0, PAIRS):
                            pe.wait_ge(h_made, k + 1 if prior is None else GN.after(u, k + 1))
                        last = three(bank[:, :], (wh[:, k, cols], wl[:, k, cols]),
                                     (h_hi[:, k, n * NH:(n + 1) * NH], h_lo[:, k, n * NH:(n + 1) * NH]), k, KT)
                    last.then_inc(filled["act"], 1)
                elif kind == "max":
                    s = STACK[a % HEADS]
                    t, half = divmod(n, HALVES)
                    mm(bank[:, :], q_hh[s][0:D, t * P:(t + 1) * P], k_hl[s][0:D, half * NH:(half + 1) * NH],
                       start=True, stop=True).then_inc(filled["dve"], 1)
                elif kind == "mrow":
                    for t in range(JT // HALVES):
                        last = mm(bank[0:1, t * P:(t + 1) * P], mcol[:, n * 4 + t:n * 4 + t + 1], ident_r[:, :],
                                  start=True, stop=True)
                    last.then_inc(filled["act"], 1)
                elif kind == "den":
                    for c in range(QUARTERS):
                        last = mm(bank[c * QP:(c + 1) * QP, 0:QN], ones[:, :], sum_pool[:, c * QN:(c + 1) * QN],
                                  start=True, stop=True)
                    last.then_inc(filled["act"], 1)
                elif kind == "gm":
                    mm(bank[:, 0:1], group_avg[:, :], meanvar[:, 0:1], start=True, stop=True).then_inc(filled["dve"], 1)
                elif kind == "gv":
                    mm(bank[:, 0:1], group_avg[:, :], spread_sq[:, :], start=True, stop=True).then_inc(filled["dve"], 1)
                elif kind == "v":
                    for k in range(KT):
                        wh, wl = w_tiles(WV0 if k < 2 else WV1)
                        tok = slice(a * P, (a + 1) * P)
                        last = three(bank[:, :], (wh[:, k % 2, :], wl[:, k % 2, :]),
                                     (h_hi[:, k, tok], h_lo[:, k, tok]), k, KT, flip=True)
                    last.then_inc(filled["act"], 1)
                elif kind == "out":
                    wh, wl = w_tiles(WO0 if a < 2 else WO1)
                    cols = slice(a % 2 * P, (a % 2 + 1) * P)
                    for k in range(KT):
                        half = slice(n * NH, (n + 1) * NH)
                        last = three(bank[:, :], (wh[:, k, cols], wl[:, k, cols]), (o_hi[:, k, half], o_lo[:, k, half]), k, KT)
                    last.then_inc(filled["dve"], 1)

            pe.wait_ge(consts_pool, 4)
            pe.wait_ge(consts_dve, 4)
            for item in pro_items:
                kind, a, n = item
                if kind == "gm":
                    pe.wait_ge(stats_made, a + 1)
                elif kind == "gv":
                    pe.wait_ge(spread_made, a + 1)
                elif kind == "q" and n == 0:
                    pe.wait_ge(w_split, 1)
                elif kind == "v" and a == 0:
                    pe.wait_ge(w_split, PRO)
                elif kind == "max" and n == 0:
                    pe.wait_ge(dve_drained, drained(pro_items[:pro_items.index(item)], "dve"))
                elif kind == "mrow":
                    pe.wait_ge(maxima_made, n + 1)
                fill(pro_items, item, None, 0)

            def unit(u, last):
                items, slots = unit_items(last), unit_slots(last)

                def prior(who, n):
                    return DRAINED[who].after(u, n)

                def scores(h, j, n):
                    g, s = (h * JT + j) * HALVES + n, STACK[h]
                    if h % 2 == 0 and j == 0 and n == 0:
                        pe.wait_ge(hi_copied, QKS.after(u, 4 * (h // 2)))
                    if g >= BANKS:
                        pe.wait_ge(exps_done, HALF_STEPS.after(u, g - BANKS + 1))
                    out, keys, half = s_ps[g % BANKS][:, :], slice(j * P, (j + 1) * P), slice(n * NH, (n + 1) * NH)
                    mm(out, k_hl[s][:, keys], q_hh[s][:, half], start=True, stop=False)
                    if j == 0:
                        upto = items[:items.index(("mrow", h, n)) + 1] if h > 0 else []
                        pe.wait_ge(act_drained, DRAINED["act"].after(u, drained(upto, "act")))
                    mm(out, k_h1[s][:, keys], q_lm[s][:, half], start=False, stop=True).then_inc(scores_made, 1)

                def values(h, j):
                    pe.wait_ge(exps_done, HALF_STEPS.after(u, (h * JT + j + 1) * HALVES))
                    if j == 0 and h >= 2:
                        pe.wait_ge(o_normed, NORMED.after(u, h - 1))
                    for half in range(HALVES):
                        done = mm(o_ps[h % 2][half * D:(half + 1) * D, :], v_sb[:, j, h * D:(h + 1) * D],
                                  probs[j % 4][:, half * NH:(half + 1) * NH], start=(j == 0), stop=(j == JT - 1))
                    done.then_inc(values_used, 1)

                def ready(item):
                    kind, a, n = item
                    if kind == "gm":
                        pe.wait_ge(stats_made, GN.after(u, a + 1))
                    elif kind == "gv":
                        pe.wait_ge(spread_made, GN.after(u, a + 1))
                    elif kind == "q" and n == 0:
                        chunk = QK_CHUNK[a % PAIRS]
                        pe.wait_ge(w_split, CHUNKS_SPLIT.after(u, chunk + 1))
                    elif kind == "max" and n == 0 and a % 2:
                        pe.wait_ge(hi_copied, QKS.after(u, 4 * (a // 2)))
                    elif kind == "max" and n < HALVES:
                        pe.wait_ge(hi_made, HIS.after(u, 2 * (4 * (a // 2 - 1) + HALVES + n + 1)))
                    elif kind == "mrow":
                        pe.wait_ge(maxima_made, MAXIMA.after(u, 2 * a - 1 + n))
                    elif kind == "den":
                        pe.wait_ge(adds_pool, ADDS["pool"].after(u, len(ADDED["pool"]) * (a + 1)))
                    elif kind == "v" and a == 0:
                        pe.wait_ge(w_split, CHUNKS_SPLIT.after(u, WV1 + 1))
                    elif kind == "out" and n == 0 and a % 2 == 0:
                        if a == 0:
                            pe.wait_ge(o_lo_made, PAIRS_SPLIT.after(u, PAIRS))
                        pe.wait_ge(w_split, CHUNKS_SPLIT.after(u, chunk_place(WO0 if a == 0 else WO1, last) + 1))

                def make(item):
                    ready(item)
                    fill(items, item, prior, u)

                for h in range(HEADS):
                    for j in range(JT):
                        before, between, behind, end = slots[h][j]
                        for item in before:
                            make(item)
                        scores(h, j, 0)
                        for item in between:
                            make(item)
                        scores(h, j, 1)
                        for item in behind:
                            make(item)
                        if j > 0:
                            values(h, j - 1)
                        elif h > 0:
                            values(h - 1, JT - 1)
                        for item in end:
                            make(item)
                values(HEADS - 1, JT - 1)
                for item in unit_tail(last):
                    make(item)

            over_units(pe, unit)


def lay_out(inputs):
    import numpy as np

    def f(name):
        return np.asarray(inputs[name])

    w1 = f("L1_conv_proj_w").reshape(HEADS, 3, D, C).transpose(1, 0, 2, 3).reshape(3 * C, C)
    b1 = f("L1_conv_proj_b").reshape(HEADS, 3, D).transpose(1, 0, 2).reshape(3 * C)
    layers = [
        (f("L0_conv_norm_w"), f("L0_conv_norm_b"), f("L0_conv_qkv_w"), f("L0_conv_qkv_b"), f("L0_conv_proj_w"), f("L0_conv_proj_b")),
        (f("L1_conv_gn_w"), f("L1_conv_gn_b"), w1, b1, f("L1_conv_out_w"), f("L1_conv_out_b")),
    ]
    weights = np.zeros((2, 8, P, 1024), np.float32)
    params = np.zeros((2, P, AHEAD + OWN), np.float32)
    for n, (gamma, beta, wqkv, bqkv, wo, bo) in enumerate(layers):
        wt = wqkv.T.reshape(KT, P, 3, C)
        for p in range(PAIRS):
            qk = wt[:, :, 0:2, p * P:(p + 1) * P]
            weights[n, p] = qk.transpose(1, 0, 2, 3).reshape(P, 1024)
        for i in range(2):
            weights[n, 4 + i] = wt[2 * i:2 * i + 2, :, 2, :].transpose(1, 0, 2).reshape(P, 1024)
            weights[n, 6 + i] = wo.T.reshape(KT, P, 2, 256)[:, :, i].transpose(1, 0, 2).reshape(P, 1024)
        bq, bk, bv = bqkv.reshape(3, PAIRS, P)
        params[n, :, GAMMA:GAMMA + KT] = gamma.reshape(KT, P).T
        params[n, :, BETA:BETA + KT] = beta.reshape(KT, P).T
        for p in range(PAIRS):
            at = 8 if p == 0 else AHEAD + 3 * (p - 1)
            params[n, :, at] = bq[p]
            params[n, :, at + 1] = bk[p]
            params[n, :D, at + 2] = bk[p, D:]
            params[n, D:, at + 2] = bk[p, :D]
        params[n, :, AHEAD + BV:AHEAD + BV + PAIRS] = bv.T
        params[n, :, AHEAD + BO:AHEAD + BO + KT] = bo.reshape(KT, P).T
    return weights, params


def kernel(**inputs):
    import numpy as np
    import concourse.bacc as bacc
    from concourse.bass_utils import run_bass_kernel_spmd as run

    x = np.asarray(inputs["x"])
    images = x.shape[0]
    weights, params = lay_out(inputs)
    arrays = {"x": x.reshape(images, C, T), "weights": weights, "params": params}
    nc = bacc.Bacc("TRN2", target_bir_lowering=False, num_devices=1)
    args = [nc.dram_tensor(n, a.shape, F32, kind="ExternalInput").ap() for n, a in arrays.items()]
    state = nc.dram_tensor("state", (3 * images, C, T), F32, kind="ExternalOutput").ap()
    build(nc, *args, state, 2 * images, images)
    r = run(nc, [arrays], core_ids=[0])
    return r.results[0]["state"][2 * images:].reshape(x.shape)
```
